# Optimizing a Trainium2 kernel written in Bass

```python
import numpy as np
import jax
import jax.numpy as jnp

def _softmax(x, axis=-1):
    return jax.nn.softmax(x, axis=axis)

def _gelu(x):
    return jax.nn.gelu(x, approximate=True)

def _silu(x):
    return jax.nn.silu(x)

def _sigmoid(x):
    return jax.nn.sigmoid(x)

def _layernorm(x, axis=-1, eps=1e-05):
    m = jnp.mean(x, axis=axis, keepdims=True)
    v = jnp.var(x, axis=axis, keepdims=True)
    return (x - m) / jnp.sqrt(v + eps)

def _scatter_add(tgt, idx, src, axis=0):
    return tgt.at[idx].add(src)

def _segment_sum(src, seg, n):
    return jax.ops.segment_sum(src, seg, n)
kernel_name = 'mk_sandwich_d1_jaxref_r8_f1924f'

def setup_inputs(seed: int=0):
    np.random.seed(seed)
    _w = jnp.asarray

    def _L0_attn_setup():
        import jax, jax.numpy as jnp
        import numpy as np
        B, T, C = (2, 256, 128)
        N_HEAD = 16
        HEAD_DIM = C // N_HEAD
        ATTN_MODE = 'local'
        LOCAL_ATTN_CTX = 32

        def build_mask(n, attn_mode, local_attn_ctx):
            i = jnp.arange(n)[:, None]
            j = jnp.arange(n)[None, :]
            causal = j <= i
            if attn_mode == 'all':
                return causal
            if attn_mode == 'local':
                return causal & (j >= i - local_attn_ctx)
            if attn_mode == 'strided':
                return causal & (j % local_attn_ctx == 0)
            raise ValueError(attn_mode)
        key = jax.random.key(seed)
        k1, k2, k3 = jax.random.split(key, 3)
        s = 0.02
        return {'x': jax.random.normal(k1, (B, T, C), dtype=jnp.float32), 'W_attn': jax.random.normal(k2, (C, 3 * C), dtype=jnp.float32) * s, 'b_attn': jnp.zeros((3 * C,), dtype=jnp.float32), 'W_proj': jax.random.normal(k3, (C, C), dtype=jnp.float32) * s, 'b_proj': jnp.zeros((C,), dtype=jnp.float32)}
    _L0_attn_in = _L0_attn_setup()

    def _L0_ffn_setup():
        import jax, jax.numpy as jnp
        import numpy as np
        DIM = 128
        DEPTH = 6
        HEADS = 16
        DIM_HEAD = 64
        WINDOW = 32
        INNER = HEADS * DIM_HEAD
        DIM_INNER = int(DIM * 4 * 2 / 3)
        QK_SCALE = 8.0

        def shift_tokens(t):
            a, s = jnp.split(t, 2, -1)
            s = jnp.pad(s, ((0, 0), (1, 0), (0, 0)))[:, :-1]
            return jnp.concatenate([a, s], -1)

        def l2norm(t):
            return t / jnp.maximum(jnp.linalg.norm(t, axis=-1, keepdims=True), 1e-12)

        def rotate_half(x):
            x1, x2 = jnp.split(x, 2, -1)
            return jnp.concatenate([-x2, x1], -1)

        def rotary_tables(n):
            half = jnp.arange(0, DIM_HEAD, 2, dtype=jnp.float32)
            inv_freq = 1.0 / 10000.0 ** (half / DIM_HEAD)
            t = jnp.arange(n, dtype=jnp.float32)
            freqs = t[:, None] * inv_freq[None, :]
            freqs = jnp.concatenate([freqs, freqs], -1)
            base_scale = (half + 0.4 * DIM_HEAD) / (1.4 * DIM_HEAD)
            power = (t - n // 2) / (WINDOW // 2)
            scale = base_scale[None, :] ** power[:, None]
            scale = jnp.concatenate([scale, scale], -1)
            return (freqs, scale)

        def local_attention(q, k, v):
            b, h, n, d = q.shape
            w = WINDOW
            nw = n // w
            bq = q.reshape(b, h, nw, w, d)
            bk = k.reshape(b, h, nw, w, d)
            bv = v.reshape(b, h, nw, w, d)

            def look(t):
                p = jnp.pad(t, ((0, 0), (0, 0), (1, 0), (0, 0), (0, 0)))
                return jnp.concatenate([p[:, :, :nw], p[:, :, 1:]], axis=3)
            bk2, bv2 = (look(bk), look(bv))
            seq = jnp.arange(n).reshape(nw, w)
            seq_p = jnp.pad(seq, ((1, 0), (0, 0)), constant_values=-1)
            jt = jnp.concatenate([seq_p[:nw], seq_p[1:]], axis=1)
            it = seq[:, :, None]
            jb = jt[:, None, :]
            mask = (it < jb) | (it > jb + w) | (jb == -1)
            sim = jnp.einsum('bhwie,bhwje->bhwij', bq, bk2) * QK_SCALE
            sim = jnp.where(mask, -jnp.finfo(sim.dtype).max, sim)
            attn = jax.nn.softmax(sim, -1)
            out = jnp.einsum('bhwij,bhwje->bhwie', attn, bv2)
            return out.reshape(b, h, n, d)

        def attn_layer(x, Wqkv, qs, ksc, Wo):
            b, n, _ = x.shape
            qkv = x @ Wqkv
            q, k, v = jnp.split(qkv, 3, -1)
            sh = lambda t: t.reshape(b, n, HEADS, DIM_HEAD).transpose(0, 2, 1, 3)
            q, k, v = (sh(q), sh(k), sh(v))
            q = l2norm(q) * qs
            k = l2norm(k) * ksc
            freqs, scale = rotary_tables(n)
            cos, sin = (jnp.cos(freqs), jnp.sin(freqs))
            q = q * cos * scale + rotate_half(q) * sin * scale
            inv = 1.0 / scale
            k = k * cos * inv + rotate_half(k) * sin * inv
            out = local_attention(q, k, v)
            out = out.transpose(0, 2, 1, 3).reshape(b, n, INNER)
            return out @ Wo

        def ffn_layer(x, g, bln, W1, b1, W2, b2):
            mu = x.mean(-1, keepdims=True)
            var = ((x - mu) ** 2).mean(-1, keepdims=True)
            xn = (x - mu) / jnp.sqrt(var + 1e-05) * g + bln
            hg = xn @ W1 + b1
            a, gate = jnp.split(hg, 2, -1)
            return a * jax.nn.gelu(gate, approximate=False) @ W2 + b2
        key = jax.random.key(seed)
        ks = jax.random.split(key, 8)
        B, N = (2, 256)
        init = lambda k, shape: jax.random.normal(k, shape, jnp.float32) * 0.02
        return {'x': jax.random.normal(ks[0], (B, N, DIM), jnp.float32), 'Wqkv': init(ks[1], (DEPTH, DIM, 3 * INNER)), 'q_scale': jnp.ones((DEPTH, DIM_HEAD), jnp.float32), 'k_scale': jnp.ones((DEPTH, DIM_HEAD), jnp.float32), 'Wo': init(ks[2], (DEPTH, INNER, DIM)), 'ln_g': jnp.ones((DEPTH, DIM), jnp.float32), 'ln_b': jnp.zeros((DEPTH, DIM), jnp.float32), 'W1': init(ks[3], (DEPTH, DIM, 2 * DIM_INNER)), 'b1': jnp.zeros((DEPTH, 2 * DIM_INNER), jnp.float32), 'W2': init(ks[4], (DEPTH, DIM_INNER, DIM)), 'b2': jnp.zeros((DEPTH, DIM), jnp.float32)}
    _L0_ffn_in = _L0_ffn_setup()
    _d = {'L0_attn_x': _L0_attn_in['x'], 'L0_attn_W_attn': _L0_attn_in['W_attn'], 'L0_attn_b_attn': _L0_attn_in['b_attn'], 'L0_attn_W_proj': _L0_attn_in['W_proj'], 'L0_attn_b_proj': _L0_attn_in['b_proj'], 'L0_ffn_Wqkv': _L0_ffn_in['Wqkv'], 'L0_ffn_q_scale': _L0_ffn_in['q_scale'], 'L0_ffn_k_scale': _L0_ffn_in['k_scale'], 'L0_ffn_Wo': _L0_ffn_in['Wo'], 'L0_ffn_ln_g': _L0_ffn_in['ln_g'], 'L0_ffn_ln_b': _L0_ffn_in['ln_b'], 'L0_ffn_W1': _L0_ffn_in['W1'], 'L0_ffn_b1': _L0_ffn_in['b1'], 'L0_ffn_W2': _L0_ffn_in['W2'], 'L0_ffn_b2': _L0_ffn_in['b2']}
    _x0 = _d['L0_attn_x']
    _d['L0_attn_x'] = jax.random.normal(jax.random.fold_in(jax.random.key(seed), 1), (2, 1024, 128), dtype=_x0.dtype)
    del _x0
    return _d

def reference(L0_attn_x, L0_attn_W_attn, L0_attn_b_attn, L0_attn_W_proj, L0_attn_b_proj, L0_ffn_Wqkv, L0_ffn_q_scale, L0_ffn_k_scale, L0_ffn_Wo, L0_ffn_ln_g, L0_ffn_ln_b, L0_ffn_W1, L0_ffn_b1, L0_ffn_W2, L0_ffn_b2):

    def _L0_attn_ref(x, W_attn, b_attn, W_proj, b_proj):
        import jax, jax.numpy as jnp
        import numpy as np
        B, T, C = (2, 256, 128)
        N_HEAD = 16
        HEAD_DIM = C // N_HEAD
        ATTN_MODE = 'local'
        LOCAL_ATTN_CTX = 32

        def build_mask(n, attn_mode, local_attn_ctx):
            i = jnp.arange(n)[:, None]
            j = jnp.arange(n)[None, :]
            causal = j <= i
            if attn_mode == 'all':
                return causal
            if attn_mode == 'local':
                return causal & (j >= i - local_attn_ctx)
            if attn_mode == 'strided':
                return causal & (j % local_attn_ctx == 0)
            raise ValueError(attn_mode)
        b, t, c = x.shape
        qkv = x @ W_attn + b_attn
        q, k, v = jnp.split(qkv, 3, axis=-1)

        def heads(a):
            return a.reshape(b, t, N_HEAD, HEAD_DIM).transpose(0, 2, 1, 3)
        q, k, v = (heads(q), heads(k), heads(v))
        scale = 1.0 / np.sqrt(HEAD_DIM)
        scores = jnp.einsum('bhtd,bhsd->bhts', q, k) * scale
        mask = build_mask(t, ATTN_MODE, LOCAL_ATTN_CTX)
        scores = jnp.where(mask[None, None], scores, -jnp.inf)
        attn = jax.nn.softmax(scores, axis=-1)
        out = jnp.einsum('bhts,bhsd->bhtd', attn, v)
        out = out.transpose(0, 2, 1, 3).reshape(b, t, c)
        return out @ W_proj + b_proj

    def _L0_ffn_ref(x, Wqkv, q_scale, k_scale, Wo, ln_g, ln_b, W1, b1, W2, b2):
        import jax, jax.numpy as jnp
        import numpy as np
        DIM = 128
        DEPTH = 6
        HEADS = 16
        DIM_HEAD = 64
        WINDOW = 32
        INNER = HEADS * DIM_HEAD
        DIM_INNER = int(DIM * 4 * 2 / 3)
        QK_SCALE = 8.0

        def shift_tokens(t):
            a, s = jnp.split(t, 2, -1)
            s = jnp.pad(s, ((0, 0), (1, 0), (0, 0)))[:, :-1]
            return jnp.concatenate([a, s], -1)

        def l2norm(t):
            return t / jnp.maximum(jnp.linalg.norm(t, axis=-1, keepdims=True), 1e-12)

        def rotate_half(x):
            x1, x2 = jnp.split(x, 2, -1)
            return jnp.concatenate([-x2, x1], -1)

        def rotary_tables(n):
            half = jnp.arange(0, DIM_HEAD, 2, dtype=jnp.float32)
            inv_freq = 1.0 / 10000.0 ** (half / DIM_HEAD)
            t = jnp.arange(n, dtype=jnp.float32)
            freqs = t[:, None] * inv_freq[None, :]
            freqs = jnp.concatenate([freqs, freqs], -1)
            base_scale = (half + 0.4 * DIM_HEAD) / (1.4 * DIM_HEAD)
            power = (t - n // 2) / (WINDOW // 2)
            scale = base_scale[None, :] ** power[:, None]
            scale = jnp.concatenate([scale, scale], -1)
            return (freqs, scale)

        def local_attention(q, k, v):
            b, h, n, d = q.shape
            w = WINDOW
            nw = n // w
            bq = q.reshape(b, h, nw, w, d)
            bk = k.reshape(b, h, nw, w, d)
            bv = v.reshape(b, h, nw, w, d)

            def look(t):
                p = jnp.pad(t, ((0, 0), (0, 0), (1, 0), (0, 0), (0, 0)))
                return jnp.concatenate([p[:, :, :nw], p[:, :, 1:]], axis=3)
            bk2, bv2 = (look(bk), look(bv))
            seq = jnp.arange(n).reshape(nw, w)
            seq_p = jnp.pad(seq, ((1, 0), (0, 0)), constant_values=-1)
            jt = jnp.concatenate([seq_p[:nw], seq_p[1:]], axis=1)
            it = seq[:, :, None]
            jb = jt[:, None, :]
            mask = (it < jb) | (it > jb + w) | (jb == -1)
            sim = jnp.einsum('bhwie,bhwje->bhwij', bq, bk2) * QK_SCALE
            sim = jnp.where(mask, -jnp.finfo(sim.dtype).max, sim)
            attn = jax.nn.softmax(sim, -1)
            out = jnp.einsum('bhwij,bhwje->bhwie', attn, bv2)
            return out.reshape(b, h, n, d)

        def attn_layer(x, Wqkv, qs, ksc, Wo):
            b, n, _ = x.shape
            qkv = x @ Wqkv
            q, k, v = jnp.split(qkv, 3, -1)
            sh = lambda t: t.reshape(b, n, HEADS, DIM_HEAD).transpose(0, 2, 1, 3)
            q, k, v = (sh(q), sh(k), sh(v))
            q = l2norm(q) * qs
            k = l2norm(k) * ksc
            freqs, scale = rotary_tables(n)
            cos, sin = (jnp.cos(freqs), jnp.sin(freqs))
            q = q * cos * scale + rotate_half(q) * sin * scale
            inv = 1.0 / scale
            k = k * cos * inv + rotate_half(k) * sin * inv
            out = local_attention(q, k, v)
            out = out.transpose(0, 2, 1, 3).reshape(b, n, INNER)
            return out @ Wo

        def ffn_layer(x, g, bln, W1, b1, W2, b2):
            mu = x.mean(-1, keepdims=True)
            var = ((x - mu) ** 2).mean(-1, keepdims=True)
            xn = (x - mu) / jnp.sqrt(var + 1e-05) * g + bln
            hg = xn @ W1 + b1
            a, gate = jnp.split(hg, 2, -1)
            return a * jax.nn.gelu(gate, approximate=False) @ W2 + b2
        for i in range(DEPTH):
            x = attn_layer(shift_tokens(x), Wqkv[i], q_scale[i], k_scale[i], Wo[i]) + x
            x = ffn_layer(shift_tokens(x), ln_g[i], ln_b[i], W1[i], b1[i], W2[i], b2[i]) + x
        return x
    x = L0_attn_x
    x = x + _layernorm(_L0_attn_ref(_layernorm(x, axis=-1), L0_attn_W_attn, L0_attn_b_attn, L0_attn_W_proj, L0_attn_b_proj), axis=-1)
    x = x + _layernorm(_L0_ffn_ref(_layernorm(x, axis=-1), L0_ffn_Wqkv, L0_ffn_q_scale, L0_ffn_k_scale, L0_ffn_Wo, L0_ffn_ln_g, L0_ffn_ln_b, L0_ffn_W1, L0_ffn_b1, L0_ffn_W2, L0_ffn_b2), axis=-1)
    return x

_drawn_inputs = setup_inputs


def setup_inputs(seed=0):
    import zlib

    import numpy as np

    out = dict(_drawn_inputs(seed))
    spreads = {'L0_attn_b_attn': (0.0, 0.1),
     'L0_attn_b_proj': (0.0, 0.1),
     'L0_ffn_q_scale': (1.0, 0.6),
     'L0_ffn_k_scale': (1.0, 0.6),
     'L0_ffn_ln_g': (1.0, 0.6),
     'L0_ffn_ln_b': (0.0, 0.8),
     'L0_ffn_b1': (0.0, 0.8),
     'L0_ffn_b2': (0.0, 0.1)}
    factors = {'L0_ffn_W1': 4.384, 'L0_ffn_W2': 4.117}
    for name, (base, spread) in spreads.items():
        noise = np.random.default_rng([zlib.crc32(name.encode()), seed]).standard_normal(out[name].shape)
        drawn = base * np.exp(spread * noise) if base else spread * noise
        out[name] = jnp.asarray(drawn.astype(out[name].dtype))
    for name, factor in factors.items():
        out[name] = (out[name] * factor).astype(out[name].dtype)
    return out
```

```python
import concourse.bass as bass
from concourse import mybir
from contextlib import ExitStack

B, N, C, P = 2, 1024, 128, 128
TILES = B * N // P
PER_SEQ = N // P
DEPTH, HEADS, WIN = 6, 16, 32
D = 64
DA = C // HEADS
INNER = HEADS * D
FF = int(C * 4 * 2 / 3)
KEYS = WIN + P
FF_CHUNKS = [(0, 128), (128, 128), (256, FF - 256)]
CHUNKS = HEADS // 2
SUPER = 4
SUPERS = TILES // SUPER
HB = 8 * D
PAR = 9
EPS = 1e-5


class Stage:

    def __init__(self, first):
        self.first = first
        self.K = DA if first else D
        self.turn = [0, 1, 2, 3, 4, 5, 6, 7] if first else [0, 1, 2, 3, 4, 5, 7, 8]
        self.out_turn = [None, 8] if first else [6, 9]

    def heads(self, c):
        if self.first:
            return 32 * (c // 2), [(g, 4 * g + c // 2) for g in (2 * (c % 2), 2 * (c % 2) + 1)]
        return 64 * (c % 2), [(g, 2 * g + c % 2) for g in (2 * (c // 2), 2 * (c // 2) + 1)]

    def column(self, head):
        return head * DA if self.first else (head % 8) * D


FIRST, LAYER = Stage(True), Stage(False)


def build(nc, x, Wa, ba, Wp, bp, Wqkv, Wo, scales, W1, W2, par, rope, ident, identb, mask, out):
    f32, bf16 = mybir.dt.float32, mybir.dt.bfloat16
    ALU, ACT, AX = mybir.AluOpType, mybir.ActivationFunctionType, mybir.AxisListType
    ctx = ExitStack()
    with ctx:
        def sb(name, shape, dt=f32):
            return ctx.enter_context(nc.sbuf_tensor(name, shape, dt))

        def sem(name):
            return ctx.enter_context(nc.semaphore(name))

        x_nat = sb("x_nat", [P, TILES, C])
        y_nat = sb("y_nat", [P, TILES, C])
        ln_nat = sb("ln_nat", [P, TILES, C])
        xA = sb("xA", [C, TILES + 1, P + 1])
        xB = sb("xB", [C, TILES + 1, P + 1])
        wa = sb("wa", [C, 3 * C])
        wp = sb("wp", [C, C])
        bias_a = sb("bias_a", [P, 3 * C])
        bias_p = sb("bias_p", [P, C])
        wqkv = sb("wqkv", [C, 3 * INNER])
        wo = sb("wo", [P, CHUNKS, C])
        w1 = sb("w1", [C, 2 * FF])
        w2 = sb("w2", [P, 3, C])
        vec = sb("vec", [P, PAR])
        scl = sb("scl", [P, 4, D])
        rope0 = sb("rope0", [P, 4, PER_SEQ, D])
        ropeL = sb("ropeL", [P, 4, TILES, D])
        idf = sb("idf", [P, P])
        idb = sb("idb", [P, P], mybir.dt.uint16)
        msk = sb("msk", [P, TILES, KEYS], mybir.dt.uint16)
        follows = sb("follows", [P, TILES])
        half_neg = sb("half_neg", [P, TILES])
        xs = sb("xs", [C, 2, P])
        sq = sb("sq", [P, 2, HB])
        n2 = sb("n2", [P, 2, 8])
        n2c = sb("n2c", [P, 2, 8])
        rn = sb("rn", [P, 2, 8])
        tc_ = sb("tc_", [P, 2, HB])
        ts_ = sb("ts_", [P, 2, HB])
        tsum = sb("tsum", [P, 2, HB])
        w_nat = sb("w_nat", [P, 2, HB])
        qT = sb("qT", [P, 2, 8, P])
        kT = sb("kT", [P, 2, 8, KEYS])
        v = sb("v", [P, 2, INNER])
        vprev = sb("vprev", [WIN, 2, INNER])
        nmax = sb("nmax", [P, 2, HEADS])
        prob = sb("prob", [P, 2, 2, KEYS])
        lsum = sb("lsum", [P, 2, HEADS])
        linv = sb("linv", [P, 2, HEADS])
        pT = sb("pT", [P, 2, 2, P])
        pTprev = sb("pTprev", [WIN, 2, 2, WIN])
        o_nat = sb("o_nat", [P, 2, HB])
        oT = sb("oT", [P, 2, HB])
        xf = sb("xf", [C, 2, SUPER, P])
        xn = sb("xn", [P, SUPER, C])
        xnT = sb("xnT", [C, SUPER * P])
        gl = sb("gl", [P, 2, SUPER * P])
        hid = sb("hid", [P, 3, SUPER * P])
        stats = sb("stats", [P, TILES, 6])
        mv = sb("mv", [P, TILES, 2])
        veps = sb("veps", [P, TILES])
        rstd = sb("rstd", [P, TILES])

        bank = [ctx.enter_context(nc.psum_tensor(f"bank{i}", [P, 512], f32)) for i in range(8)]
        PJ, SB, PT, OB, TP, YB = bank[0:2], bank[2:4], bank[4], bank[5], bank[6], bank[7]

        phase = sem("phase")
        x_loaded, c_loaded = sem("x_loaded"), sem("c_loaded")
        att_loaded, ffn_loaded = sem("att_loaded"), sem("ffn_loaded")
        init_done = sem("init_done")
        rope_ready = sem("rope_ready")
        xs_ready = sem("xs_ready")
        pj_ready = sem("pj_ready")
        pj_act = sem("pj_act")
        pj_dve = sem("pj_dve")
        n2_ready = sem("n2_ready")
        pool_step = sem("pool_step")
        w_ready = sem("w_ready")
        tp_full, tp_free = sem("tp_full"), sem("tp_free")
        prev_ready = sem("prev_ready")
        s_ready = sem("s_ready")
        max_ready = sem("max_ready")
        p_ready = sem("p_ready")
        pt_full, pt_free = sem("pt_full"), sem("pt_free")
        pv_done = sem("pv_done")
        linv_ready = sem("linv_ready")
        o_evac = sem("o_evac")
        wo_done = sem("wo_done")
        y_free = sem("y_free")
        a_qkv = sem("a_qkv")
        a_pj = sem("a_pj")
        ln_step, ln_pow = sem("ln_step"), sem("ln_pow")
        lnT_full, lnT_free = sem("lnT_full"), sem("lnT_free")
        f_x, f_t1, f_st, f_eps, f_pow, f_xn, f_t2, f_xnT = (sem(n) for n in (
            "f_x", "f_t1", "f_st", "f_eps", "f_pow", "f_xn", "f_t2", "f_xnT"))
        f_gate, f_act, f_up, f_hid, f_down, f_out = (sem(n) for n in (
            "f_gate", "f_act", "f_up", "f_hid", "f_down", "f_out"))
        out_ready, out_stored = sem("out_ready"), sem("out_stored")

        CONSTS = 16 * 8

        def at_least(eng, s, value):
            if not (isinstance(value, int) and value <= 0):
                eng.wait_ge(s, value)

        def begin(eng, k):
            at_least(eng, phase, 4 * k)

        def end(eng):
            eng.drain().then_inc(phase, 1)

        LAST = 3 + 2 * DEPTH

        def tiles(eng, tile, base, first_static):
            i0 = 0
            if first_static:
                tile(base, 0, 0, True)
                tile(base + 1, 1, 1, True)
                i0 = 1
            with eng.Fori(i0, TILES // 2 - 1) as i:
                tile(base + i * 2, i * 2, 0, True)
                tile(base + i * 2 + 1, i * 2 + 1, 1, True)
            tile(base + TILES - 2, TILES - 2, 0, True)
            tile(base + TILES - 1, TILES - 1, 1, False)

        block = ctx.enter_context(nc.Block())

        @block.sync
        def _(eng):
            for s in range(SUPERS):
                eng.dma_start(x_nat[:, s * SUPER:(s + 1) * SUPER, :],
                              x[s * SUPER * P:(s + 1) * SUPER * P, :].rearrange("(t p) c -> p t c", p=P)
                              ).then_inc(x_loaded, 16)
            for dst, src in ((idf[:, :], ident), (idb[:, :], identb), (wa[:, :], Wa), (wp[:, :], Wp),
                             (bias_a[:, :], ba), (bias_p[:, :], bp), (msk[:, :, :], mask),
                             (rope0[:, :, :, :], rope)):
                eng.dma_start(dst, src).then_inc(c_loaded, 16)
            for l in range(DEPTH):
                if l:
                    eng.wait_ge(phase, 4 * (2 + 2 * l))
                eng.dma_start(wqkv[:, :], Wqkv[l, :, :]).then_inc(att_loaded, 16)
                eng.dma_start(wo[:, :, :], Wo[l, :, :].rearrange("(i p) c -> p i c", p=P)).then_inc(att_loaded, 16)
                eng.dma_start(scl[:, :, :], scales[l, :, :, :]).then_inc(att_loaded, 16)
                if l:
                    eng.wait_ge(phase, 4 * (3 + 2 * l))
                eng.dma_start(w1[:, :], W1[l, :, :]).then_inc(ffn_loaded, 16)
                eng.dma_start(w2[:, :, :], W2[l, :, :].rearrange("(i p) c -> p i c", p=P)).then_inc(ffn_loaded, 16)
                eng.dma_start(vec[:, :], par[l, :, :]).then_inc(ffn_loaded, 16)
            for s in range(SUPERS):
                eng.wait_ge(out_ready, s + 1)
                eng.dma_start(out[s * SUPER * P:(s + 1) * SUPER * P, :].rearrange("(t p) c -> p t c", p=P),
                              x_nat[:, s * SUPER:(s + 1) * SUPER, :]).then_inc(out_stored, 16)
            eng.wait_ge(out_stored, 16 * SUPERS)

        @block.gpsimd
        def _(eng):
            nc.gpsimd.memset(half_neg[:, :], -0.5).then_inc(init_done, 1)
            nc.gpsimd.memset(w_nat[:, :, :], 0.0).then_inc(init_done, 1)
            nc.gpsimd.memset(kT[:, :, :, :], 0.0).then_inc(init_done, 1)
            nc.gpsimd.memset(v[:, :, :], 0.0).then_inc(init_done, 1)
            nc.gpsimd.memset(xA[:, :, :], 0.0).then_inc(init_done, 1)
            nc.gpsimd.memset(xB[:, :, :], 0.0).then_inc(init_done, 1)
            nc.gpsimd.memset(follows[:, :], 1.0).then_inc(init_done, 1)
            eng.wait_ge(init_done, 7)
            nc.gpsimd.memset(follows[:, 0:TILES:PER_SEQ], 0.0).then_inc(init_done, 1)
            eng.wait_ge(init_done, 8)

            def pow_rstd(k):
                eng.wait_ge(ln_step, 2 * k + 1)
                nc.gpsimd.tensor_tensor(rstd[:, :], veps[:, :], half_neg[:, :], ALU.pow).then_inc(ln_pow, 1)

            def rotate(q_idx):
                for j in range(4):
                    r, Q = j % 2, q_idx + j
                    eng.wait_ge(pj_dve, Q + 1)
                    nc.gpsimd.tensor_tensor(tsum[:, r, :], tc_[:, r, :], ts_[:, r, :], ALU.add)
                    nc.gpsimd.tensor_scalar(n2c[:, r, :], n2[:, r, :], 1e-24, None, ALU.max).then_inc(pool_step, 1)
                    eng.wait_ge(pool_step, 2 * Q + 1)
                    nc.gpsimd.tensor_tensor(rn[:, r, :], n2c[:, r, :], half_neg[:, 0:8], ALU.pow).then_inc(pool_step, 1)
                    eng.wait_ge(pool_step, 2 * Q + 2)
                    at_least(eng, tp_free, 2 * TILES + Q - 1)
                    nc.gpsimd.tensor_tensor(
                        w_nat[:, r, :].rearrange("p (h d) -> p h d", d=D), tsum[:, r, :].rearrange("p (h d) -> p h d", d=D),
                        rn[:, r, :].rearrange("p (h o) -> p h o", o=1).to_broadcast([P, 8, D]), ALU.mult).then_inc(w_ready, 1)

            pow_rstd(0)
            end(eng)
            begin(eng, 1)
            end(eng)
            begin(eng, 2)
            pow_rstd(1)
            pow_rstd(2)
            end(eng)
            with eng.Fori(0, DEPTH) as l:
                begin(eng, 3 + l * 2)
                eng.wait_ge(c_loaded, CONSTS)
                eng.wait_ge(att_loaded, (l + 1) * 48)
                for k in range(4):
                    nc.gpsimd.tensor_tensor(
                        ropeL[:, k, :, :].rearrange("p (b t) d -> p b (t d)", b=B),
                        rope0[:, k, :, :].rearrange("p (o t) d -> p o (t d)", o=1).to_broadcast([P, B, PER_SEQ * D]),
                        ropeS(scl, k, P, B), ALU.mult).then_inc(rope_ready, 1)
                rotate(l * (TILES * 4))

                def tile(t, n, p, has_next):
                    if has_next:
                        rotate((t - TILES + 1) * 4)
                tiles(eng, tile, TILES + l * TILES, False)
                end(eng)
                begin(eng, 4 + l * 2)
                for s in range(SUPERS):
                    F = l * SUPERS + s
                    eng.wait_ge(f_eps, F + 1)
                    nc.gpsimd.tensor_tensor(rstd[:, 0:SUPER], veps[:, 0:SUPER], half_neg[:, 0:SUPER], ALU.pow
                                            ).then_inc(f_pow, 1)
                end(eng)
            begin(eng, LAST)
            pow_rstd(3)

        @block.scalar
        def _(eng):
            def lnT(k):
                for s in range(SUPERS):
                    K = k * SUPERS + s
                    eng.wait_ge(lnT_full, K + 1)
                    src = bank[s][:, :].rearrange("p (t q) -> p t q", t=SUPER)
                    tl = slice(s * SUPER, (s + 1) * SUPER)
                    nc.scalar.activation(xA[:, tl, 1:P + 1], src, ACT.Copy)
                    for j in range(SUPER):
                        n = s * SUPER + j + 1
                        if n % PER_SEQ:
                            nc.scalar.activation(xA[:, n, 0:1], src[:, j, P - 1:P], ACT.Copy)

            def copy_input(n, p, shift):
                lo = C // 2
                nc.scalar.activation(xs[0:lo, p, :], xA[0:lo, n, 1:P + 1], ACT.Copy).then_inc(xs_ready, 1)
                a = 0 if shift else 1
                nc.scalar.activation(xs[lo:C, p, :], xA[lo:C, n, a:P + a], ACT.Copy).then_inc(xs_ready, 1)

            def shifted(l, s):
                lo, tl = C // 2, slice(s * SUPER, (s + 1) * SUPER)
                if s >= 2:
                    eng.wait_ge(f_t1, l * SUPERS + s - 1)
                nc.scalar.activation(xf[0:lo, s % 2, :, :], xB[0:lo, tl, 1:P + 1], ACT.Copy).then_inc(f_x, 1)
                nc.scalar.activation(xf[lo:C, s % 2, :, :], xB[lo:C, tl, 0:P], ACT.Copy).then_inc(f_x, 1)

            def exps(t, p, c):
                st = stage[0]
                G, r = t * 8 + c, c % 2
                eng.wait_ge(max_ready, G + 1)
                at_least(eng, pt_full, t * 10 + st.turn[c - 2] + 1 if c >= 2 else (t - 1) * 10 + st.turn[c + 6] + 1)
                for h, (g, head) in enumerate(st.heads(c)[1]):
                    last = nc.scalar.activation(
                        prob[:, r, h, :], SB[r][:, h * KEYS:(h + 1) * KEYS], ACT.Exp,
                        bias=nmax[:, p, 2 * c + h:2 * c + h + 1], accum_out=lsum[:, p, head:head + 1])
                last.then_inc(p_ready, 1)

            def square(t, j, fresh=False):
                J, Q = (t - TILES) * 6 + j, (t - TILES) * 4 + j
                eng.wait_ge(pj_ready, J + 1)
                if not (fresh and j < 2):
                    eng.wait_ge(n2_ready, Q - 1)
                nc.scalar.activation(sq[:, j % 2, :], PJ[j % 2][:, :], ACT.Square).then_inc(pj_act, 1)

            def values(t, p, j):
                J = (t - TILES) * 6 + j
                eng.wait_ge(pj_ready, J + 1)
                eng.wait_ge(pv_done, (t - 1) * 8)
                eng.wait_ge(prev_ready, t * 2)
                nc.scalar.activation(v[:, p, (j - 4) * HB:(j - 3) * HB], PJ[j % 2][:, :], ACT.Copy).then_inc(pj_act, 1)

            def heads_T(t, p, j):
                Q = 2 * TILES + (t - TILES) * 4 + j
                eng.wait_ge(tp_full, Q + 1)
                eng.wait_ge(s_ready, (t - 1) * 8)
                eng.wait_ge(prev_ready, t * 2)
                src = TP[:, :].rearrange("p (g q) -> p g q", g=4)
                g0 = 4 * (j // 2)
                dst = qT[:, p, g0:g0 + 4, :] if j % 2 == 0 else kT[:, p, g0:g0 + 4, WIN:KEYS]
                nc.scalar.activation(dst, src, ACT.Copy).then_inc(tp_free, 1)

            def heads_T_first(t, p, j):
                at_least(eng, s_ready, (t - 1) * 8)
                at_least(eng, prev_ready, t * 2)
                eng.wait_ge(tp_full, t * 2 + j + 1)
                src = TP[:, :].rearrange("p (g q) -> p g q", g=4)
                dst = qT[:, p, 0:4, :] if j == 0 else kT[:, p, 0:4, WIN:KEYS]
                nc.scalar.activation(dst, src, ACT.Copy, scale=DA ** -0.5 if j == 0 else 1.0).then_inc(tp_free, 1)

            stage = [FIRST]
            eng.wait_ge(init_done, 8)
            lnT(0)
            end(eng)
            begin(eng, 1)
            copy_input(0, 0, False)
            heads_T_first(0, 0, 0)
            heads_T_first(0, 0, 1)

            def tile_first(t, n, p, has_next):
                if has_next:
                    copy_input(n + 1, 1 - p, False)
                for c in range(CHUNKS):
                    exps(t, p, c)
                    if has_next and c in (4, 5):
                        heads_T_first(t + 1, 1 - p, c - 4)
            tiles(eng, tile_first, 0, True)
            end(eng)
            begin(eng, 2)
            lnT(1)
            end(eng)
            stage[0] = LAYER
            with eng.Fori(0, DEPTH) as l:
                begin(eng, 3 + l * 2)
                t0 = TILES + l * TILES
                copy_input(0, 0, True)
                square(t0, 0, True)
                square(t0, 1, True)
                square(t0, 2, True)
                heads_T(t0, 0, 0)
                square(t0, 3, True)
                heads_T(t0, 0, 1)
                values(t0, 0, 4)
                heads_T(t0, 0, 2)
                values(t0, 0, 5)
                heads_T(t0, 0, 3)

                def tile(t, n, p, has_next):
                    if has_next:
                        copy_input(n + 1, 1 - p, True)
                    for c in range(CHUNKS):
                        exps(t, p, c)
                        if has_next:
                            if c < 4:
                                square(t + 1, c)
                            if 3 <= c < 7:
                                heads_T(t + 1, 1 - p, c - 3)
                            if c == 4:
                                values(t + 1, 1 - p, 4)
                            if c == 7:
                                values(t + 1, 1 - p, 5)
                tiles(eng, tile, t0, False)
                end(eng)
                begin(eng, 4 + l * 2)
                shifted(l, 0)
                eng.wait_ge(ffn_loaded, (l + 1) * 48)
                for s in range(SUPERS):
                    F = l * SUPERS + s
                    if s + 1 < SUPERS:
                        shifted(l, s + 1)
                    eng.wait_ge(f_t2, F + 1)
                    if s:
                        eng.wait_ge(f_up, F * 3)
                    nc.scalar.activation(xnT[:, :], bank[1][:, :], ACT.Identity, scale=vec[:, 0:1],
                                         bias=vec[:, 1:2]).then_inc(f_xnT, 1)
                    for i, (_, m) in enumerate(FF_CHUNKS):
                        k = F * 3 + i
                        r = (s * 3 + i) % 2
                        eng.wait_ge(f_gate, k + 1)
                        if s * 3 + i >= 2:
                            eng.wait_ge(f_hid, k - 1)
                        nc.scalar.activation(gl[0:m, r, :], bank[2 + r][0:m, :], ACT.Gelu,
                                             bias=vec[0:m, 5 + i:6 + i]).then_inc(f_act, 1)
                end(eng)
            begin(eng, LAST)
            for s in range(SUPERS):
                eng.wait_ge(lnT_full, 2 * SUPERS + s + 1)
                nc.scalar.activation(y_nat[:, s * SUPER:(s + 1) * SUPER, :],
                                     bank[s][:, :].rearrange("p (t q) -> p t q", t=SUPER), ACT.Copy
                                     ).then_inc(lnT_free, 1)

        @block.vector
        def _(eng):
            def norms(src, k, tl=range(TILES)):
                for n in tl:
                    last = nc.vector.bn_stats(stats[:, n, :], src[:, n, :])
                last.then_inc(f_st, 1)
                eng.wait_ge(f_st, fst[0])
                fst[0] += 1
                for n in tl:
                    last = nc.vector.bn_aggr(mv[:, n, :], stats[:, n, :])
                last.then_inc(f_st, 1)
                eng.wait_ge(f_st, fst[0])
                fst[0] += 1
                nc.vector.tensor_scalar(veps[:, :], mv[:, :, 1], EPS, None, ALU.add).then_inc(ln_step, 1)
                eng.wait_ge(ln_pow, k + 1)
                for n in tl:
                    last = nc.vector.tensor_scalar(ln_nat[:, n, :], src[:, n, :], mv[:, n, 0:1], rstd[:, n:n + 1],
                                                   ALU.subtract, ALU.mult)
                last.then_inc(ln_step, 1)

            fst = [1]

            def maxima(t, p, c):
                G, r = t * 8 + c, c % 2
                eng.wait_ge(s_ready, G + 1)
                if c == 0:
                    at_least(eng, p_ready, (t - 1) * 8)
                nc.vector.tensor_reduce(nmax[:, p, 2 * c:2 * c + 2],
                                        SB[r][:, 0:2 * KEYS].rearrange("p (h k) -> p h k", h=2),
                                        AX.X, ALU.max, negate=True).then_inc(max_ready, 1)

            def probs_T(t, c):
                G, r = t * 8 + c, c % 2
                eng.wait_ge(pt_full, t * 10 + stage[0].turn[c] + 1)
                at_least(eng, pv_done, G - 1)
                nc.vector.tensor_copy(pT[:, r, :, :], PT[:, 0:2 * P].rearrange("p (h q) -> p h q", h=2))
                nc.vector.tensor_copy(pTprev[:, r, :, :],
                                      PT[0:WIN, 2 * P:2 * P + 2 * WIN].rearrange("p (h q) -> p h q", h=2)
                                      ).then_inc(pt_free, 1)

            def heads_out(t, p, half):
                st = stage[0]
                H = t * 2 + half
                eng.wait_ge(pv_done, t * 8 + 4 * half + 4)
                at_least(eng, pt_full, (t - 1) * 10 + [7, 10][half])
                hs = slice(0, HEADS) if st.first else slice(8 * half, 8 * half + 8)
                nc.vector.reciprocal(linv[:, p, hs], lsum[:, p, hs]).then_inc(linv_ready, 1)
                eng.wait_ge(linv_ready, t + 1 if st.first else H - TILES + 1)
                w, nh = (DA, HEADS) if st.first else (D, 8)
                nc.vector.tensor_tensor(
                    o_nat[:, half, 0:w * nh].rearrange("p (h d) -> p h d", d=w),
                    OB[:, 0:w * nh].rearrange("p (h d) -> p h d", d=w),
                    linv[:, p, hs].rearrange("p (h o) -> p h o", o=1).to_broadcast([P, nh, w]),
                    ALU.mult).then_inc(o_evac, 2 if st.first else 1)

            def heads_out_T(t, half):
                eng.wait_ge(pt_full, t * 10 + [7, 10][half])
                at_least(eng, wo_done, (t - 1) * 2 + half + 1)
                m = P if stage[0].first else HB
                nc.vector.tensor_copy(oT[:, half, 0:m], PT[:, 0:m]).then_inc(pt_free, 2 if stage[0].first else 1)

            def residual(t, n):
                eng.wait_ge(wo_done, t * 2 + 2)
                if stage[0].first:
                    nc.vector.tensor_tensor(y_nat[:, n, :], YB[:, 0:C], bias_p[:, :], ALU.add).then_inc(y_free, 1)
                else:
                    nc.vector.tensor_tensor(xB[:, n + 1, 0:1], YB[:, P - 1:P], xA[:, n, P:P + 1], ALU.add)
                    nc.vector.tensor_tensor(xB[:, n, 1:P + 1], YB[:, 0:P], xA[:, n, 1:P + 1], ALU.add
                                            ).then_inc(y_free, 1)

            def copy_prev(t, n, p):
                at_least(eng, s_ready, (t - 1) * 8)
                at_least(eng, pv_done, (t - 1) * 8)
                nc.vector.tensor_scalar(kT[:, p, :, 0:WIN], kT[:, 1 - p, :, P:KEYS], follows[:, bass.ds(n, 1)], None, ALU.mult).then_inc(prev_ready, 1)
                nc.vector.tensor_copy(vprev[:, p, :], v[P - WIN:P, 1 - p, :]).then_inc(prev_ready, 1)

            def rotary(t, n, j, fresh=False):
                i = t - TILES
                J, Q, r = i * 6 + j, i * 4 + j, j % 2
                eng.wait_ge(pj_act, J + 1)
                if not (fresh and j < 2):
                    eng.wait_ge(w_ready, Q - 1)
                heads3 = "p (h d) -> p h d"
                nc.vector.tensor_reduce(n2[:, r, :], sq[:, r, :].rearrange(heads3, d=D), AX.X, ALU.add
                                        ).then_inc(n2_ready, 1)
                k = 2 * (j % 2)
                nc.vector.tensor_tensor(
                    tc_[:, r, :].rearrange(heads3, d=D), PJ[r][:, :].rearrange(heads3, d=D),
                    ropeL[:, k, n, :].rearrange("p (o d) -> p o d", o=1).to_broadcast([P, 8, D]), ALU.mult)
                for a in range(2):
                    lo, hi = a * (D // 2), (1 - a) * (D // 2)
                    last = nc.vector.tensor_tensor(
                        ts_[:, r, :].rearrange(heads3, d=D)[:, :, lo:lo + D // 2],
                        PJ[r][:, :].rearrange(heads3, d=D)[:, :, hi:hi + D // 2],
                        ropeL[:, k + 1, n, lo:lo + D // 2].rearrange("p (o d) -> p o d", o=1
                                                                     ).to_broadcast([P, 8, D // 2]), ALU.mult)
                last.then_inc(pj_dve, 1)

            def qkv_first(t, p):
                eng.wait_ge(a_pj, t + 1)
                at_least(eng, tp_free, t * 2)
                at_least(eng, pv_done, (t - 1) * 8)
                at_least(eng, prev_ready, t * 2)
                for j in range(2):
                    nc.vector.tensor_tensor(
                        w_nat[:, j, :].rearrange("p (h d) -> p h d", d=32)[:, :, 0:DA],
                        PJ[0][:, j * C:(j + 1) * C].rearrange("p (h d) -> p h d", d=DA),
                        bias_a[:, j * C:(j + 1) * C].rearrange("p (h d) -> p h d", d=DA), ALU.add).then_inc(a_qkv, 1)
                nc.vector.tensor_tensor(v[:, p, 0:C], PJ[0][:, 2 * C:3 * C], bias_a[:, 2 * C:3 * C], ALU.add
                                        ).then_inc(a_qkv, 1)

            stage = [FIRST]
            eng.wait_ge(x_loaded, 16 * SUPERS)
            norms(x_nat, 0)
            end(eng)
            begin(eng, 1)
            eng.wait_ge(c_loaded, CONSTS)
            copy_prev(0, 0, 0)
            qkv_first(0, 0)
            maxima(0, 0, 0)
            maxima(0, 0, 1)

            def tile_first(t, n, p, has_next):
                for c in range(CHUNKS):
                    probs_T(t, c)
                    if c < CHUNKS - 2:
                        maxima(t, p, c + 2)
                    if has_next and c == 1:
                        eng.wait_ge(a_qkv, t * 3 + 3)
                        copy_prev(t + 1, n + 1, 1 - p)
                    if has_next and c == 2:
                        qkv_first(t + 1, 1 - p)
                heads_out(t, p, 1)
                if has_next:
                    maxima(t + 1, 1 - p, 0)
                heads_out_T(t, 1)
                if has_next:
                    maxima(t + 1, 1 - p, 1)
                residual(t, n)
            tiles(eng, tile_first, 0, True)
            end(eng)
            begin(eng, 2)
            norms(y_nat, 1)
            eng.wait_ge(ln_step, 4)
            for n in range(TILES):
                last = nc.vector.tensor_tensor(x_nat[:, n, :], x_nat[:, n, :], ln_nat[:, n, :], ALU.add)
            last.then_inc(f_st, 1)
            eng.wait_ge(f_st, fst[0])
            fst[0] += 1
            norms(x_nat, 2)
            end(eng)
            stage[0] = LAYER
            base_st = fst[0] - 1
            with eng.Fori(0, DEPTH) as l:
                begin(eng, 3 + l * 2)
                t0 = TILES + l * TILES
                eng.wait_ge(rope_ready, l * 4 + 4)
                rotary(t0, 0, 0, True)
                rotary(t0, 0, 1, True)
                rotary(t0, 0, 2, True)
                rotary(t0, 0, 3, True)
                copy_prev(t0, 0, 0)
                maxima(t0, 0, 0)
                maxima(t0, 0, 1)

                def tile(t, n, p, has_next):
                    for c in range(CHUNKS):
                        probs_T(t, c)
                        if c < CHUNKS - 2:
                            maxima(t, p, c + 2)
                        if c == 3:
                            heads_out(t, p, 0)
                        if c == 5:
                            heads_out_T(t, 0)
                        if has_next and c < 4:
                            rotary(t + 1, n + 1, c)
                        if has_next and c == 0:
                            eng.wait_ge(pj_act, (t - TILES) * 6 + 6)
                            eng.wait_ge(tp_free, 2 * TILES + (t - TILES) * 4 + 4)
                            copy_prev(t + 1, n + 1, 1 - p)
                    heads_out(t, p, 1)
                    if has_next:
                        maxima(t + 1, 1 - p, 0)
                    heads_out_T(t, 1)
                    if has_next:
                        maxima(t + 1, 1 - p, 1)
                    residual(t, n)
                tiles(eng, tile, t0, False)
                eng.wait_ge(y_free, t0 + TILES)
                nc.vector.memset(xB[:, PER_SEQ, 0:1], 0.0)
                end(eng)
                begin(eng, 4 + l * 2)
                eng.wait_ge(ffn_loaded, (l + 1) * 48)
                for s in range(SUPERS):
                    F = l * SUPERS + s
                    eng.wait_ge(f_t1, F + 1)
                    for j in range(SUPER):
                        last = nc.vector.bn_stats(stats[:, j, :], bank[0][:, j * C:(j + 1) * C])
                    eng.drain()
                    for j in range(SUPER):
                        last = nc.vector.bn_aggr(mv[:, j, :], stats[:, j, :])
                    last.then_inc(f_st, 1)
                    eng.wait_ge(f_st, F + 1 + base_st)
                    nc.vector.tensor_scalar(veps[:, 0:SUPER], mv[:, 0:SUPER, 1], EPS, None, ALU.add).then_inc(f_eps, 1)
                    eng.wait_ge(f_pow, F + 1)
                    if s:
                        eng.wait_ge(f_t2, F)
                    for j in range(SUPER):
                        last = nc.vector.tensor_scalar(xn[:, j, :], bank[0][:, j * C:(j + 1) * C], mv[:, j, 0:1],
                                                       rstd[:, j:j + 1], ALU.subtract, ALU.mult)
                    last.then_inc(f_xn, 1)
                    for i, (_, m) in enumerate(FF_CHUNKS):
                        k = F * 3 + i
                        r = (s * 3 + i) % 2
                        eng.wait_ge(f_act, k + 1)
                        eng.wait_ge(f_up, k + 1)
                        if s and i == 0:
                            eng.wait_ge(f_down, F)
                        nc.vector.scalar_tensor_tensor(hid[0:m, i, :], bank[4 + r][0:m, :], vec[0:m, 2 + i:3 + i],
                                                       gl[0:m, r, :], ALU.add, ALU.mult).then_inc(f_hid, 1)
                    eng.wait_ge(f_down, F + 1)
                    y4 = bank[6][:, :].rearrange("p (t q) -> p t q", t=SUPER)
                    t4 = slice(s * SUPER, (s + 1) * SUPER)
                    nc.vector.scalar_tensor_tensor(xA[:, s * SUPER + 1:(s + 1) * SUPER + 1, 0:1], y4[:, :, P - 1:P],
                                                   vec[:, 8:9], xB[:, t4, P:P + 1], ALU.add, ALU.add)
                    nc.vector.scalar_tensor_tensor(xA[:, t4, 1:P + 1], y4, vec[:, 8:9], xB[:, t4, 1:P + 1],
                                                   ALU.add, ALU.add).then_inc(f_out, 1)
                eng.wait_ge(f_out, (l + 1) * SUPERS)
                nc.vector.memset(xA[:, PER_SEQ, 0:1], 0.0)
                end(eng)
            begin(eng, LAST)
            eng.wait_ge(lnT_free, SUPERS)
            for n in range(TILES):
                last = nc.vector.bn_stats(stats[:, n, :], y_nat[:, n, :])
            last.then_inc(f_st, 1)
            at = base_st + DEPTH * SUPERS
            eng.wait_ge(f_st, at + 1)
            for n in range(TILES):
                last = nc.vector.bn_aggr(mv[:, n, :], stats[:, n, :])
            last.then_inc(f_st, 1)
            eng.wait_ge(f_st, at + 2)
            nc.vector.tensor_scalar(veps[:, :], mv[:, :, 1], EPS, None, ALU.add).then_inc(ln_step, 1)
            eng.wait_ge(ln_pow, 4)
            for n in range(TILES):
                last = nc.vector.tensor_scalar(ln_nat[:, n, :], y_nat[:, n, :], mv[:, n, 0:1], rstd[:, n:n + 1],
                                               ALU.subtract, ALU.mult)
            last.then_inc(f_st, 1)
            eng.wait_ge(f_st, at + 3)
            for s in range(SUPERS):
                t4 = slice(s * SUPER, (s + 1) * SUPER)
                nc.vector.tensor_tensor(x_nat[:, t4, :], x_nat[:, t4, :], ln_nat[:, t4, :], ALU.add).then_inc(out_ready, 1)

        @block.tensor
        def _(eng):
            def transposes(src, k):
                for s in range(SUPERS):
                    for j in range(SUPER):
                        last = nc.tensor.transpose(bank[s][:, j * P:(j + 1) * P], src(s * SUPER + j), idf[:, :])
                    last.then_inc(lnT_full, 1)

            def scores(t, n, p, c):
                st = stage[0]
                G, r = t * 8 + c, c % 2
                base, pair = st.heads(c)
                if c == 0:
                    eng.wait_ge(tp_free, t * 2 + 2 if st.first else 2 * TILES + (t - TILES) * 4 + 4)
                    eng.wait_ge(prev_ready, t * 2 + 2)
                at_least(eng, p_ready, G - 1)
                nc.tensor.matmul(SB[r][:, 0:2 * KEYS], idb[:, :].bitcast(bf16),
                                 msk[:, n, :].bitcast(bf16).rearrange("p (o k) -> p o k", o=1).to_broadcast([P, 2, KEYS]),
                                 start=True, stop=False, skip_group_check=True)
                for h, (g, head) in enumerate(pair):
                    last = nc.tensor.matmul(SB[r][:, h * KEYS:(h + 1) * KEYS], qT[base:base + st.K, p, g, :],
                                            kT[base:base + st.K, p, g, :], start=False, stop=True,
                                            skip_group_check=True)
                last.then_inc(s_ready, 1)

            def transpose_probs(t, c):
                G, r = t * 8 + c, c % 2
                eng.wait_ge(p_ready, G + 1)
                at_least(eng, pt_free, t * 10 + stage[0].turn[c])
                for h in range(2):
                    nc.tensor.transpose(PT[:, h * P:(h + 1) * P], prob[:, r, h, WIN:KEYS], idf[:, :])
                for h in range(2):
                    last = nc.tensor.transpose(PT[0:WIN, 2 * P + h * WIN:2 * P + (h + 1) * WIN],
                                               prob[0:WIN, r, h, 0:WIN], idf[0:WIN, 0:WIN])
                last.then_inc(pt_full, 1)

            def weigh_values(t, p, c):
                st = stage[0]
                eng.wait_ge(pt_free, t * 10 + stage[0].turn[c] + 1)
                if c == 0:
                    at_least(eng, o_evac, t * 2)
                    if st.first:
                        eng.wait_ge(a_qkv, t * 3 + 3)
                    else:
                        eng.wait_ge(pj_act, (t - TILES) * 6 + 6)
                if c == 4 and not st.first:
                    eng.wait_ge(o_evac, t * 2 + 1)
                r = c % 2
                for h, (g, head) in enumerate(st.heads(c)[1]):
                    a, vc = st.column(head), slice(head * st.K, (head + 1) * st.K)
                    nc.tensor.matmul(OB[:, a:a + st.K], pT[:, r, h, :], v[:, p, vc], start=True, stop=False,
                                     skip_group_check=True)
                    last = nc.tensor.matmul(OB[0:WIN, a:a + st.K], pTprev[:, r, h, :], vprev[:, p, vc],
                                            start=False, stop=True, skip_group_check=True)
                last.then_inc(pv_done, 1)

            def project(t, p, j, fresh=False):
                i = t - TILES
                J = i * 6 + j
                if j == 0:
                    eng.wait_ge(xs_ready, t * 2 + 2)
                if not (fresh and j < 2):
                    eng.wait_ge(pj_act, J - 1)
                if j >= 2:
                    eng.wait_ge(pj_dve, i * 4 + j - 1)
                col = [0, INNER, HB, INNER + HB, 2 * INNER, 2 * INNER + HB][j]
                nc.tensor.matmul(PJ[j % 2][:, :], xs[:, p, :], wqkv[:, col:col + HB], start=True, stop=True
                                 ).then_inc(pj_ready, 1)

            def transpose_heads(t, j):
                Q = (t - TILES) * 4 + j
                eng.wait_ge(w_ready, Q + 1)
                eng.wait_ge(tp_free, 2 * TILES + Q)
                for i in range(4):
                    last = nc.tensor.transpose(TP[:, i * P:(i + 1) * P], w_nat[:, j % 2, i * P:(i + 1) * P], idf[:, :])
                last.then_inc(tp_full, 1)

            def project_first(t, p):
                eng.wait_ge(xs_ready, t * 2 + 2)
                at_least(eng, a_qkv, t * 3)
                nc.tensor.matmul(PJ[0][:, 0:3 * C], xs[:, p, :], wa[:, :], start=True, stop=True).then_inc(a_pj, 1)

            def transpose_first(t, j):
                eng.wait_ge(a_qkv, t * 3 + j + 1)
                at_least(eng, tp_free, t * 2 + j)
                for i in range(4):
                    last = nc.tensor.transpose(TP[:, i * P:(i + 1) * P], w_nat[:, j, i * P:(i + 1) * P], idf[:, :])
                last.then_inc(tp_full, 1)

            def transpose_out(t, half):
                st = stage[0]
                eng.wait_ge(o_evac, t * 2 + half + 1)
                eng.wait_ge(pt_free, t * 10 + st.out_turn[half])
                for i in range(1 if st.first else 4):
                    last = nc.tensor.transpose(PT[:, i * P:(i + 1) * P], o_nat[:, half, i * P:(i + 1) * P], idf[:, :])
                last.then_inc(pt_full, 2 if st.first else 1)

            def project_out(t, half):
                st = stage[0]
                eng.wait_ge(pt_free, t * 10 + [7, 10][half])
                if half == 0 or st.first:
                    at_least(eng, y_free, t)
                if st.first:
                    nc.tensor.matmul(YB[:, 0:C], oT[:, 1, 0:P], wp[:, :], start=True, stop=True).then_inc(wo_done, 2)
                    return
                for i in range(4):
                    last = nc.tensor.matmul(YB[:, 0:P], wo[:, 4 * half + i, :], oT[:, half, i * P:(i + 1) * P],
                                            start=half == 0 and i == 0, stop=half == 1 and i == 3)
                last.then_inc(wo_done, 1)

            stage = [FIRST]
            eng.wait_ge(c_loaded, CONSTS)
            eng.wait_ge(ln_step, 2)
            transposes(lambda n: ln_nat[:, n, :], 0)
            end(eng)
            begin(eng, 1)
            project_first(0, 0)
            transpose_first(0, 0)
            transpose_first(0, 1)
            scores(0, 0, 0, 0)
            scores(0, 0, 0, 1)

            def tile_first(t, n, p, has_next):
                for c in range(CHUNKS):
                    transpose_probs(t, c)
                    if c < CHUNKS - 2:
                        scores(t, n, p, c + 2)
                    if has_next:
                        if c == 0:
                            project_first(t + 1, 1 - p)
                        if c in (3, 4):
                            transpose_first(t + 1, c - 3)
                    weigh_values(t, p, c)
                if has_next:
                    scores(t + 1, n + 1, 1 - p, 0)
                transpose_out(t, 1)
                if has_next:
                    scores(t + 1, n + 1, 1 - p, 1)
                project_out(t, 1)

            tiles(eng, tile_first, 0, True)
            end(eng)
            begin(eng, 2)
            eng.wait_ge(ln_step, 6)
            transposes(lambda n: ln_nat[:, n, :], 1)
            end(eng)
            stage[0] = LAYER
            with eng.Fori(0, DEPTH) as l:
                begin(eng, 3 + l * 2)
                eng.wait_ge(att_loaded, (l + 1) * 48)
                t0 = TILES + l * TILES
                project(t0, 0, 0, True)
                project(t0, 0, 1, True)
                project(t0, 0, 2, True)
                transpose_heads(t0, 0)
                project(t0, 0, 3, True)
                transpose_heads(t0, 1)
                project(t0, 0, 4, True)
                transpose_heads(t0, 2)
                project(t0, 0, 5, True)
                transpose_heads(t0, 3)
                scores(t0, 0, 0, 0)
                scores(t0, 0, 0, 1)

                def tile(t, n, p, has_next):
                    for c in range(CHUNKS):
                        transpose_probs(t, c)
                        if c < CHUNKS - 2:
                            scores(t, n, p, c + 2)
                        if has_next:
                            if c < 4:
                                project(t + 1, 1 - p, c)
                            if 2 <= c < 6:
                                transpose_heads(t + 1, c - 2)
                            if c == 4:
                                project(t + 1, 1 - p, 4)
                            if c == 7:
                                project(t + 1, 1 - p, 5)
                        if c == 5:
                            transpose_out(t, 0)
                        if c == 6:
                            project_out(t, 0)
                        weigh_values(t, p, c)
                    if has_next:
                        scores(t + 1, n + 1, 1 - p, 0)
                    transpose_out(t, 1)
                    if has_next:
                        scores(t + 1, n + 1, 1 - p, 1)
                    project_out(t, 1)
                tiles(eng, tile, t0, False)
                end(eng)
                begin(eng, 4 + l * 2)
                eng.wait_ge(ffn_loaded, (l + 1) * 48)
                for s in range(SUPERS):
                    F, r2 = l * SUPERS + s, s % 2
                    eng.wait_ge(f_x, F * 2 + 2)
                    if s:
                        eng.wait_ge(f_xn, F)
                    for j in range(SUPER):
                        last = nc.tensor.transpose(bank[0][:, j * C:(j + 1) * C], xf[:, r2, j, :], idf[:, :])
                    last.then_inc(f_t1, 1)
                    eng.wait_ge(f_xn, F + 1)
                    for j in range(SUPER):
                        last = nc.tensor.transpose(bank[1][:, j * P:(j + 1) * P], xn[:, j, :], idf[:, :])
                    last.then_inc(f_t2, 1)
                    eng.wait_ge(f_xnT, F + 1)
                    for i, (a, m) in enumerate(FF_CHUNKS):
                        k = F * 3 + i
                        r = (s * 3 + i) % 2
                        if s * 3 + i >= 2:
                            eng.wait_ge(f_hid, k - 1)
                        nc.tensor.matmul(bank[2 + r][0:m, :], w1[:, FF + a:FF + a + m], xnT[:, :], start=True, stop=True
                                         ).then_inc(f_gate, 1)
                        nc.tensor.matmul(bank[4 + r][0:m, :], w1[:, a:a + m], xnT[:, :], start=True, stop=True
                                         ).then_inc(f_up, 1)
                    eng.wait_ge(f_hid, F * 3 + 3)
                    if s:
                        eng.wait_ge(f_out, F)
                    for i, (_, m) in enumerate(FF_CHUNKS):
                        last = nc.tensor.matmul(bank[6][:, :], w2[0:m, i, :], hid[0:m, i, :], start=i == 0, stop=i == 2)
                    last.then_inc(f_down, 1)
                end(eng)
            begin(eng, LAST)
            transposes(lambda n: xA[:, n, 1:P + 1], 2)


def ropeS(scl, k, P, B):
    return scl[:, k, :].rearrange("p (o d) -> p o d", o=1).to_broadcast([P, B * 8, 64])


def _constants():
    import numpy as np
    f = np.float32
    half = np.arange(0, D, 2, dtype=f)
    inv_freq = (f(1.0) / f(10000.0) ** (half / f(D))).astype(f)
    t = np.arange(N, dtype=f)
    freqs = t[:, None] * inv_freq[None, :]
    freqs = np.concatenate([freqs, freqs], -1)
    base = (half + f(0.4 * D)) / f(1.4 * D)
    scale = base[None, :] ** ((t - f(N // 2)) / f(WIN // 2))[:, None]
    scale = np.concatenate([scale, scale], -1).astype(f)
    cos, sin = np.cos(freqs), np.sin(freqs)
    sign = np.concatenate([-np.ones(D // 2, f), np.ones(D // 2, f)])
    inv = f(1.0) / scale
    tabs = np.stack([cos * scale, sin * sign * scale, cos * inv * f(8), sin * sign * inv * f(8)])
    rope = tabs.reshape(4, PER_SEQ, P, D).transpose(2, 0, 1, 3).astype(f)
    i = np.arange(P)[:, None]
    j = np.arange(KEYS)[None, :] - WIN
    ok = (j <= i) & (j >= i - WIN)
    tile = np.arange(TILES)[:, None, None] % PER_SEQ
    ok = ok[None] & ((j[None] >= 0) | (tile > 0))
    mask = np.where(ok, 0.0, -1e30).transpose(1, 0, 2).astype(f)
    eye = np.eye(P, dtype=f)
    
    def bf16_bits(a):
        return (np.ascontiguousarray(a).view(np.uint32) >> 16).astype(np.uint16)
    return np.ascontiguousarray(rope), eye, bf16_bits(eye), bf16_bits(mask)


def kernel(L0_attn_x, L0_attn_W_attn, L0_attn_b_attn, L0_attn_W_proj, L0_attn_b_proj, L0_ffn_Wqkv, L0_ffn_q_scale,
           L0_ffn_k_scale, L0_ffn_Wo, L0_ffn_ln_g, L0_ffn_ln_b, L0_ffn_W1, L0_ffn_b1, L0_ffn_W2, L0_ffn_b2):
    import numpy as np
    import concourse.bacc as bacc
    from concourse.bass_utils import run_bass_kernel_spmd

    A = np.ascontiguousarray
    rope, eye, eyeb, mask = _constants()

    def swap(s):
        return np.concatenate([s[:, D // 2:], s[:, :D // 2]], -1)
    qs, ks = np.asarray(L0_ffn_q_scale), np.asarray(L0_ffn_k_scale)
    scales = np.stack([qs, swap(qs), ks, swap(ks)], 1)
    scales = A(np.broadcast_to(scales[:, None], (DEPTH, P, 4, D)))
    par = np.zeros((DEPTH, P, PAR), np.float32)
    b1 = np.asarray(L0_ffn_b1)
    par[:, :, 0], par[:, :, 1], par[:, :, 8] = np.asarray(L0_ffn_ln_g), np.asarray(L0_ffn_ln_b), np.asarray(L0_ffn_b2)
    for i, (a, m) in enumerate(FF_CHUNKS):
        par[:, :m, 2 + i] = b1[:, a:a + m]
        par[:, :m, 5 + i] = b1[:, FF + a:FF + a + m]
    w2 = np.zeros((DEPTH, 3 * P, C), np.float32)
    w2[:, :FF] = np.asarray(L0_ffn_W2)
    ins = {
        "x": A(np.asarray(L0_attn_x).reshape(B * N, C)), "w_attn": A(L0_attn_W_attn),
        "b_attn": A(np.broadcast_to(np.asarray(L0_attn_b_attn), (P, 3 * C))), "w_proj": A(L0_attn_W_proj),
        "b_proj": A(np.broadcast_to(np.asarray(L0_attn_b_proj), (P, C))), "w_qkv": A(L0_ffn_Wqkv),
        "w_o": A(L0_ffn_Wo), "scales": scales, "w_1": A(L0_ffn_W1), "w_2": w2, "vectors": par, "rope": rope,
        "identity": eye, "identity_bf16": eyeb, "mask": mask,
    }
    nc = bacc.Bacc("TRN2", target_bir_lowering=False, num_devices=1)
    aps = [nc.dram_tensor(k, a.shape, mybir.dt.from_np(a.dtype), kind="ExternalInput").ap() for k, a in ins.items()]
    out = nc.dram_tensor("out", (B * N, C), mybir.dt.float32, kind="ExternalOutput").ap()
    build(nc, *aps, out)
    r = run_bass_kernel_spmd(nc, [ins], core_ids=[0])
    return r.results[0]["out"].reshape(B, N, C)
```

```python
import concourse.bass as bass
from concourse import mybir
from contextlib import ExitStack

B, N, C, P = 2, 1024, 128, 128
TILES = B * N // P
PER_SEQ = N // P
DEPTH, HEADS, WIN = 6, 16, 32
D = 64
DA = C // HEADS
INNER = HEADS * D
FF = int(C * 4 * 2 / 3)
KEYS = WIN + P
FF_CHUNKS = [(0, 128), (128, 128), (256, FF - 256)]
CHUNKS = HEADS // 2
SUPER = 4
SUPERS = TILES // SUPER
HB = 8 * D
PAR = 9
EPS = 1e-5


class Stage:

    def __init__(self, first):
        self.first = first
        self.K = DA if first else D
        self.half = 8 * self.K

    def heads(self, c):
        if self.first:
            return 0, [(2 * c, 2 * c), (2 * c + 1, 2 * c + 1)]
        return 64 * (c % 2), [(g, 2 * g + c % 2) for g in (2 * (c // 2), 2 * (c // 2) + 1)]

    def column(self, head):
        return (head % 8) * self.K


def turn(t, c, opening):
    return t * 10 + (c - (0 if opening else 1) if c < 3 else c if c < 7 else 8)


def out_turn(t, half, closing):
    return t * 10 + (7 if half == 0 else 9 if closing else 12)


QK_AT, V_AT = [0, 1, 2, 4], [3, 5]
PROJECT = {0: 0, 1: 1, 3: 2, 4: 3, 5: 4, 7: 5}
SQUARE = {0: 0, 1: 1, 3: 2, 5: 3}
ROTARY = {1: 0, 2: 1, 4: 2, 6: 3}
VALUES = {4: 0, 7: 1}
LATE = (3, 7)
HEADS_T = {3: 0, 5: 1, 7: 2}

FIRST, LAYER = Stage(True), Stage(False)


def build(nc, x, Wa, ba, Wp, bp, Wqkv, Wo, scales, W1, W2, par, rope, ident, identb, mask, select, out):
    f32, bf16 = mybir.dt.float32, mybir.dt.bfloat16
    ALU, ACT, AX = mybir.AluOpType, mybir.ActivationFunctionType, mybir.AxisListType
    ctx = ExitStack()
    with ctx:
        def sb(name, shape, dt=f32):
            return ctx.enter_context(nc.sbuf_tensor(name, shape, dt))

        def sem(name):
            return ctx.enter_context(nc.semaphore(name))

        x_nat = sb("x_nat", [P, TILES, C])
        y_nat = sb("y_nat", [P, TILES, C])
        ln_nat = sb("ln_nat", [P, TILES, C])
        xA = sb("xA", [C, TILES + 1, P + 1])
        xB = sb("xB", [C, TILES + 1, P + 1])
        wa = sb("wa", [C, 3 * C])
        wp = sb("wp", [C // 2, 2, C])
        bias_a = sb("bias_a", [P, 3 * C])
        bias_p = sb("bias_p", [P, C])
        wqkv = sb("wqkv", [C, 3 * INNER])
        wo = sb("wo", [P, CHUNKS, C])
        w1 = sb("w1", [C, 2 * FF])
        w2 = sb("w2", [P, 3, C])
        vec = sb("vec", [P, PAR])
        scl = sb("scl", [P, 4, D])
        rope0 = sb("rope0", [P, 4, PER_SEQ, D])
        ropeL = sb("ropeL", [P, 4, TILES, D])
        idf = sb("idf", [P, P])
        idb = sb("idb", [P, P], mybir.dt.uint16)
        sel = sb("sel", [P, HEADS])
        kEach = sb("kEach", [P, 2, HEADS, KEYS])
        msk = sb("msk", [P, TILES, KEYS], mybir.dt.uint16)
        follows = sb("follows", [P, TILES])
        half_neg = sb("half_neg", [P, TILES])
        xs = sb("xs", [C, 2, P])
        sq = sb("sq", [P, 2, HB])
        n2 = sb("n2", [P, 2, 8])
        n2c = sb("n2c", [P, 2, 8])
        rn = sb("rn", [P, 2, 8])
        tc_ = sb("tc_", [P, 2, HB])
        ts_ = sb("ts_", [P, 2, HB])
        tsum = sb("tsum", [P, 2, HB])
        w_nat = sb("w_nat", [P, 2, HB])
        qT = sb("qT", [P, 2, 8, P])
        kT = sb("kT", [P, 2, 8, KEYS])
        v = sb("v", [P, 2, INNER])
        vprev = sb("vprev", [WIN, 2, INNER])
        nmax = sb("nmax", [P, 2, HEADS])
        prob = sb("prob", [P, 2, 2, KEYS])
        lsum = sb("lsum", [P, 2, HEADS])
        linv = sb("linv", [P, 2, HEADS])
        pT = sb("pT", [P, 2, 2, P])
        pTprev = sb("pTprev", [WIN, 2, 2, WIN])
        o_nat = sb("o_nat", [P, 2, HB])
        oT = sb("oT", [P, 2, HB])
        xf = sb("xf", [C, 2, SUPER, P])
        xn = sb("xn", [P, SUPER, C])
        xnT = sb("xnT", [C, SUPER * P])
        gl = sb("gl", [P, 2, SUPER * P])
        hid = sb("hid", [P, 3, SUPER * P])
        stats = sb("stats", [P, TILES, 6])
        mv = sb("mv", [P, TILES, 2])
        veps = sb("veps", [P, TILES])
        rstd = sb("rstd", [P, TILES])

        bank = [ctx.enter_context(nc.psum_tensor(f"bank{i}", [P, 512], f32)) for i in range(8)]
        PJ, SB, PT, OB, TP, YB = bank[0:2], bank[2:4], bank[4], bank[5], bank[6], bank[7]

        phase = sem("phase")
        x_loaded, c_loaded = sem("x_loaded"), sem("c_loaded")
        att_loaded, ffn_loaded = sem("att_loaded"), sem("ffn_loaded")
        init_done = sem("init_done")
        rope_ready = sem("rope_ready")
        xs_ready = sem("xs_ready")
        pj_ready = sem("pj_ready")
        pj_act = sem("pj_act")
        pj_dve = sem("pj_dve")
        n2_ready = sem("n2_ready")
        pool_step = sem("pool_step")
        w_ready = sem("w_ready")
        tp_full, tp_free = sem("tp_full"), sem("tp_free")
        prev_ready = sem("prev_ready")
        s_ready = sem("s_ready")
        max_ready = sem("max_ready")
        p_ready = sem("p_ready")
        pt_full, pt_free = sem("pt_full"), sem("pt_free")
        pv_done = sem("pv_done")
        linv_ready = sem("linv_ready")
        o_evac = sem("o_evac")
        wo_done = sem("wo_done")
        y_free = sem("y_free")
        a_qkv = sem("a_qkv")
        k_each = sem("k_each")
        a_pj = sem("a_pj")
        ln_step, ln_pow = sem("ln_step"), sem("ln_pow")
        lnT_full, lnT_free = sem("lnT_full"), sem("lnT_free")
        f_x, f_t1, f_st, f_eps, f_pow, f_xn, f_t2, f_xnT = (sem(n) for n in (
            "f_x", "f_t1", "f_st", "f_eps", "f_pow", "f_xn", "f_t2", "f_xnT"))
        f_gate, f_act, f_up, f_hid, f_down, f_out = (sem(n) for n in (
            "f_gate", "f_act", "f_up", "f_hid", "f_down", "f_out"))
        out_ready, out_stored = sem("out_ready"), sem("out_stored")

        CONSTS = 16 * 9

        def at_least(eng, s, value):
            if not (isinstance(value, int) and value <= 0):
                eng.wait_ge(s, value)

        def begin(eng, k):
            at_least(eng, phase, 4 * k)

        def end(eng):
            eng.drain().then_inc(phase, 1)

        LAST = 3 + 2 * DEPTH

        def tiles(eng, tile, close, base):
            tile(base, 0, 0, True, False)
            tile(base + 1, 1, 1, False, False)
            with eng.Fori(1, TILES // 2 - 1) as i:
                tile(base + i * 2, i * 2, 0, False, False)
                tile(base + i * 2 + 1, i * 2 + 1, 1, False, False)
            tile(base + TILES - 2, TILES - 2, 0, False, False)
            tile(base + TILES - 1, TILES - 1, 1, False, True)
            close(base + TILES - 1, TILES - 1, 1)

        block = ctx.enter_context(nc.Block())

        @block.sync
        def _(eng):
            for s in range(SUPERS):
                eng.dma_start(x_nat[:, s * SUPER:(s + 1) * SUPER, :],
                              x[s * SUPER * P:(s + 1) * SUPER * P, :].rearrange("(t p) c -> p t c", p=P)
                              ).then_inc(x_loaded, 16)
            for dst, src in ((idf[:, :], ident), (idb[:, :], identb), (wa[:, :], Wa), (wp[:, :, :], Wp.rearrange("(h p) c -> p h c", h=2)),
                             (bias_a[:, :], ba), (bias_p[:, :], bp), (msk[:, :, :], mask),
                             (rope0[:, :, :, :], rope), (sel[:, :], select)):
                eng.dma_start(dst, src).then_inc(c_loaded, 16)
            for l in range(DEPTH):
                if l:
                    eng.wait_ge(phase, 4 * (2 + 2 * l))
                eng.dma_start(wqkv[:, :], Wqkv[l, :, :]).then_inc(att_loaded, 16)
                eng.dma_start(wo[:, :, :], Wo[l, :, :].rearrange("(i p) c -> p i c", p=P)).then_inc(att_loaded, 16)
                eng.dma_start(scl[:, :, :], scales[l, :, :, :]).then_inc(att_loaded, 16)
                if l:
                    eng.wait_ge(phase, 4 * (3 + 2 * l))
                eng.dma_start(w1[:, :], W1[l, :, :]).then_inc(ffn_loaded, 16)
                eng.dma_start(w2[:, :, :], W2[l, :, :].rearrange("(i p) c -> p i c", p=P)).then_inc(ffn_loaded, 16)
                eng.dma_start(vec[:, :], par[l, :, :]).then_inc(ffn_loaded, 16)
            for s in range(SUPERS):
                eng.wait_ge(out_ready, s + 1)
                eng.dma_start(out[s * SUPER * P:(s + 1) * SUPER * P, :].rearrange("(t p) c -> p t c", p=P),
                              x_nat[:, s * SUPER:(s + 1) * SUPER, :]).then_inc(out_stored, 16)
            eng.wait_ge(out_stored, 16 * SUPERS)

        @block.gpsimd
        def _(eng):
            nc.gpsimd.memset(half_neg[:, :], -0.5).then_inc(init_done, 1)
            nc.gpsimd.memset(w_nat[:, :, :], 0.0).then_inc(init_done, 1)
            nc.gpsimd.memset(kT[:, :, :, :], 0.0).then_inc(init_done, 1)
            nc.gpsimd.memset(v[:, :, :], 0.0).then_inc(init_done, 1)
            nc.gpsimd.memset(xA[:, :, :], 0.0).then_inc(init_done, 1)
            nc.gpsimd.memset(xB[:, :, :], 0.0).then_inc(init_done, 1)
            nc.gpsimd.memset(o_nat[:, :, 0:P], 0.0).then_inc(init_done, 1)
            nc.gpsimd.memset(follows[:, :], 1.0).then_inc(init_done, 1)
            eng.wait_ge(init_done, 8)
            nc.gpsimd.memset(follows[:, 0:TILES:PER_SEQ], 0.0).then_inc(init_done, 1)
            eng.wait_ge(init_done, 9)

            def pow_rstd(k):
                eng.wait_ge(ln_step, 2 * k + 1)
                nc.gpsimd.tensor_tensor(rstd[:, :], veps[:, :], half_neg[:, :], ALU.pow).then_inc(ln_pow, 1)

            def rotate(q_idx):
                for j in range(4):
                    r, Q = j % 2, q_idx + j
                    eng.wait_ge(pj_dve, Q + 1)
                    nc.gpsimd.tensor_tensor(tsum[:, r, :], tc_[:, r, :], ts_[:, r, :], ALU.add)
                    nc.gpsimd.tensor_scalar(n2c[:, r, :], n2[:, r, :], 1e-24, None, ALU.max).then_inc(pool_step, 1)
                    eng.wait_ge(pool_step, 2 * Q + 1)
                    nc.gpsimd.tensor_tensor(rn[:, r, :], n2c[:, r, :], half_neg[:, 0:8], ALU.pow).then_inc(pool_step, 1)
                    eng.wait_ge(pool_step, 2 * Q + 2)
                    at_least(eng, tp_free, TILES + Q - 1)
                    nc.gpsimd.tensor_tensor(
                        w_nat[:, r, :].rearrange("p (h d) -> p h d", d=D), tsum[:, r, :].rearrange("p (h d) -> p h d", d=D),
                        rn[:, r, :].rearrange("p (h o) -> p h o", o=1).to_broadcast([P, 8, D]), ALU.mult).then_inc(w_ready, 1)

            pow_rstd(0)
            end(eng)
            begin(eng, 1)

            def split_keys(t, p):
                for c in range(CHUNKS):
                    if c == 0:
                        eng.wait_ge(tp_free, t + 1)
                        eng.wait_ge(prev_ready, t * 2 + 2)
                    nc.gpsimd.tensor_tensor(
                        kEach[:, p, 2 * c:2 * c + 2, :],
                        kT[:, p, 0, :].rearrange("p (o k) -> p o k", o=1).to_broadcast([P, 2, KEYS]),
                        sel[:, 2 * c:2 * c + 2].rearrange("p (h o) -> p h o", o=1).to_broadcast([P, 2, KEYS]),
                        ALU.mult).then_inc(k_each, 1)
            split_keys(0, 0)
            split_keys(1, 1)
            with eng.Fori(1, TILES // 2) as i:
                split_keys(i * 2, 0)
                split_keys(i * 2 + 1, 1)
            end(eng)
            begin(eng, 2)
            pow_rstd(1)
            pow_rstd(2)
            end(eng)
            with eng.Fori(0, DEPTH) as l:
                begin(eng, 3 + l * 2)
                eng.wait_ge(c_loaded, CONSTS)
                eng.wait_ge(att_loaded, (l + 1) * 48)
                for k in range(4):
                    nc.gpsimd.tensor_tensor(
                        ropeL[:, k, :, :].rearrange("p (b t) d -> p b (t d)", b=B),
                        rope0[:, k, :, :].rearrange("p (o t) d -> p o (t d)", o=1).to_broadcast([P, B, PER_SEQ * D]),
                        ropeS(scl, k, P, B), ALU.mult).then_inc(rope_ready, 1)
                rotate(l * (TILES * 4))

                with eng.Fori(1, TILES) as n:
                    rotate((l * TILES + n) * 4)
                end(eng)
                begin(eng, 4 + l * 2)
                for s in range(SUPERS):
                    F = l * SUPERS + s
                    eng.wait_ge(f_eps, F + 1)
                    nc.gpsimd.tensor_tensor(rstd[:, 0:SUPER], veps[:, 0:SUPER], half_neg[:, 0:SUPER], ALU.pow
                                            ).then_inc(f_pow, 1)
                end(eng)
            begin(eng, LAST)
            pow_rstd(3)

        @block.scalar
        def _(eng):
            def lnT(k):
                for s in range(SUPERS):
                    K = k * SUPERS + s
                    eng.wait_ge(lnT_full, K + 1)
                    src = bank[s][:, :].rearrange("p (t q) -> p t q", t=SUPER)
                    tl = slice(s * SUPER, (s + 1) * SUPER)
                    nc.scalar.activation(xA[:, tl, 1:P + 1], src, ACT.Copy)
                    for j in range(SUPER):
                        n = s * SUPER + j + 1
                        if n % PER_SEQ:
                            nc.scalar.activation(xA[:, n, 0:1], src[:, j, P - 1:P], ACT.Copy)

            def copy_input(n, p, shift):
                lo = C // 2
                nc.scalar.activation(xs[0:lo, p, :], xA[0:lo, n, 1:P + 1], ACT.Copy).then_inc(xs_ready, 1)
                a = 0 if shift else 1
                nc.scalar.activation(xs[lo:C, p, :], xA[lo:C, n, a:P + a], ACT.Copy).then_inc(xs_ready, 1)

            def shifted(l, s):
                lo, tl = C // 2, slice(s * SUPER, (s + 1) * SUPER)
                if s >= 2:
                    eng.wait_ge(f_t1, l * SUPERS + s - 1)
                nc.scalar.activation(xf[0:lo, s % 2, :, :], xB[0:lo, tl, 1:P + 1], ACT.Copy).then_inc(f_x, 1)
                nc.scalar.activation(xf[lo:C, s % 2, :, :], xB[lo:C, tl, 0:P], ACT.Copy).then_inc(f_x, 1)

            def exps(t, p, c, opening):
                st = stage[0]
                G, r = t * 8 + c, c % 2
                eng.wait_ge(max_ready, G + 1)
                at_least(eng, pt_full, (turn(t, c - 2, opening) if c >= 2 else turn(t - 1, c + 6, False)) + 1)
                for h, (g, head) in enumerate(st.heads(c)[1]):
                    last = nc.scalar.activation(
                        prob[:, r, h, :], SB[r][:, h * KEYS:(h + 1) * KEYS], ACT.Exp,
                        bias=nmax[:, p, 2 * c + h:2 * c + h + 1], accum_out=lsum[:, p, head:head + 1])
                last.then_inc(p_ready, 1)

            def square(t, j, fresh=False):
                J, Q = (t - TILES) * 6 + QK_AT[j], (t - TILES) * 4 + j
                eng.wait_ge(pj_ready, J + 1)
                if not (fresh and j < 2):
                    eng.wait_ge(n2_ready, Q - 1)
                nc.scalar.activation(sq[:, j % 2, :], PJ[QK_AT[j] % 2][:, :], ACT.Square).then_inc(pj_act, 1)

            def values(t, p, j):
                J = (t - TILES) * 6 + V_AT[j]
                eng.wait_ge(pj_ready, J + 1)
                eng.wait_ge(pv_done, (t - 1) * 8)
                eng.wait_ge(prev_ready, t * 2)
                nc.scalar.activation(v[:, p, j * HB:(j + 1) * HB], PJ[V_AT[j] % 2][:, :], ACT.Copy).then_inc(pj_act, 1)

            def heads_out_T(t, half, closing):
                eng.wait_ge(pt_full, out_turn(t, half, closing) + 1)
                at_least(eng, wo_done, (t - 1) * 2 + half + 1)
                rows, cols = (C // 2, P) if stage[0].first else (P, HB)
                nc.scalar.activation(oT[0:rows, half, 0:cols], PT[0:rows, 0:cols], ACT.Copy).then_inc(pt_free, 1)

            def heads_T(t, p, j):
                Q = TILES + (t - TILES) * 4 + j
                eng.wait_ge(tp_full, Q + 1)
                eng.wait_ge(s_ready, (t - 1) * 8)
                eng.wait_ge(prev_ready, t * 2)
                src = TP[:, :].rearrange("p (g q) -> p g q", g=4)
                g0 = 4 * (j // 2)
                dst = qT[:, p, g0:g0 + 4, :] if j % 2 == 0 else kT[:, p, g0:g0 + 4, WIN:KEYS]
                nc.scalar.activation(dst, src, ACT.Copy).then_inc(tp_free, 1)

            def heads_T_first(t, p):
                at_least(eng, s_ready, (t - 1) * 8)
                at_least(eng, prev_ready, t * 2)
                eng.wait_ge(tp_full, t + 1)
                nc.scalar.activation(qT[:, p, 0, :], TP[:, 0:P], ACT.Copy, scale=DA ** -0.5)
                nc.scalar.activation(kT[:, p, 0, WIN:KEYS], TP[:, P:2 * P], ACT.Copy).then_inc(tp_free, 1)

            stage = [FIRST]
            eng.wait_ge(init_done, 9)
            lnT(0)
            end(eng)
            begin(eng, 1)
            copy_input(0, 0, False)
            heads_T_first(0, 0)
            exps(0, 0, 0, True)

            def tile_first(t, n, p, opening, closing):
                if not closing:
                    copy_input(n + 1, 1 - p, False)
                for c in range(CHUNKS):
                    if c < CHUNKS - 1:
                        exps(t, p, c + 1, opening)
                    elif not closing:
                        exps(t + 1, 1 - p, 0, False)
                    if c == 2 and not closing:
                        heads_T_first(t + 1, 1 - p)
                    if c == 2 and not opening:
                        heads_out_T(t - 1, 1, False)
                    if c == 6:
                        heads_out_T(t, 0, False)
            tiles(eng, tile_first, lambda t, n, p: heads_out_T(t, 1, True), 0)
            end(eng)
            begin(eng, 2)
            lnT(1)
            end(eng)
            stage[0] = LAYER
            with eng.Fori(0, DEPTH) as l:
                begin(eng, 3 + l * 2)
                t0 = TILES + l * TILES
                copy_input(0, 0, True)
                square(t0, 0, True)
                square(t0, 1, True)
                square(t0, 2, True)
                values(t0, 0, 0)
                heads_T(t0, 0, 0)
                heads_T(t0, 0, 1)
                square(t0, 3, True)
                values(t0, 0, 1)
                exps(t0, 0, 0, True)

                def tile(t, n, p, opening, closing):
                    if not closing:
                        copy_input(n + 1, 1 - p, True)
                    for c in range(CHUNKS):
                        if c < CHUNKS - 1:
                            exps(t, p, c + 1, opening)
                        elif not closing:
                            exps(t + 1, 1 - p, 0, False)
                        if c == 0 and opening:
                            heads_T(t, p, 2)
                        if c == 1:
                            heads_T(t, p, 3)
                        if not closing:
                            if c in SQUARE:
                                square(t + 1, SQUARE[c])
                            if c in VALUES:
                                values(t + 1, 1 - p, VALUES[c])
                            if c in HEADS_T:
                                heads_T(t + 1, 1 - p, HEADS_T[c])
                        if c == 2 and not opening:
                            heads_out_T(t - 1, 1, False)
                        if c == 6:
                            heads_out_T(t, 0, False)
                tiles(eng, tile, lambda t, n, p: heads_out_T(t, 1, True), t0)
                end(eng)
                begin(eng, 4 + l * 2)
                shifted(l, 0)
                eng.wait_ge(ffn_loaded, (l + 1) * 48)
                for s in range(SUPERS):
                    F = l * SUPERS + s
                    if s + 1 < SUPERS:
                        shifted(l, s + 1)
                    eng.wait_ge(f_t2, F + 1)
                    if s:
                        eng.wait_ge(f_up, F * 3)
                    nc.scalar.activation(xnT[:, :], bank[1][:, :], ACT.Identity, scale=vec[:, 0:1],
                                         bias=vec[:, 1:2]).then_inc(f_xnT, 1)
                    for i, (_, m) in enumerate(FF_CHUNKS):
                        k = F * 3 + i
                        r = (s * 3 + i) % 2
                        eng.wait_ge(f_gate, k + 1)
                        if s * 3 + i >= 2:
                            eng.wait_ge(f_hid, k - 1)
                        nc.scalar.activation(gl[0:m, r, :], bank[2 + r][0:m, :], ACT.Gelu,
                                             bias=vec[0:m, 5 + i:6 + i]).then_inc(f_act, 1)
                end(eng)
            begin(eng, LAST)
            for s in range(SUPERS):
                eng.wait_ge(lnT_full, 2 * SUPERS + s + 1)
                nc.scalar.activation(y_nat[:, s * SUPER:(s + 1) * SUPER, :],
                                     bank[s][:, :].rearrange("p (t q) -> p t q", t=SUPER), ACT.Copy
                                     ).then_inc(lnT_free, 1)

        @block.vector
        def _(eng):
            def norms(src, k, tl=range(TILES)):
                for n in tl:
                    last = nc.vector.bn_stats(stats[:, n, :], src[:, n, :])
                last.then_inc(f_st, 1)
                eng.wait_ge(f_st, fst[0])
                fst[0] += 1
                for n in tl:
                    last = nc.vector.bn_aggr(mv[:, n, :], stats[:, n, :])
                last.then_inc(f_st, 1)
                eng.wait_ge(f_st, fst[0])
                fst[0] += 1
                nc.vector.tensor_scalar(veps[:, :], mv[:, :, 1], EPS, None, ALU.add).then_inc(ln_step, 1)
                eng.wait_ge(ln_pow, k + 1)
                for n in tl:
                    last = nc.vector.tensor_scalar(ln_nat[:, n, :], src[:, n, :], mv[:, n, 0:1], rstd[:, n:n + 1],
                                                   ALU.subtract, ALU.mult)
                last.then_inc(ln_step, 1)

            fst = [1]

            def maxima(t, p, c):
                G, r = t * 8 + c, c % 2
                eng.wait_ge(s_ready, G + 1)
                if c == 0:
                    at_least(eng, p_ready, (t - 1) * 8)
                nc.vector.tensor_reduce(nmax[:, p, 2 * c:2 * c + 2],
                                        SB[r][:, 0:2 * KEYS].rearrange("p (h k) -> p h k", h=2),
                                        AX.X, ALU.max, negate=True).then_inc(max_ready, 1)

            def probs_T(t, c, opening):
                G, r = t * 8 + c, c % 2
                eng.wait_ge(pt_full, turn(t, c, opening) + 1)
                at_least(eng, pv_done, G - 1)
                nc.vector.tensor_copy(pT[:, r, :, :], PT[:, 0:2 * P].rearrange("p (h q) -> p h q", h=2))
                nc.vector.tensor_copy(pTprev[:, r, :, :],
                                      PT[0:WIN, 2 * P:2 * P + 2 * WIN].rearrange("p (h q) -> p h q", h=2)
                                      ).then_inc(pt_free, 1)

            def heads_out(t, p, half):
                H, w = t * 2 + half, stage[0].K
                eng.wait_ge(pv_done, t * 8 + 4 * half + 4)
                hs = slice(8 * half, 8 * half + 8)
                nc.vector.reciprocal(linv[:, p, hs], lsum[:, p, hs]).then_inc(linv_ready, 1)
                eng.wait_ge(linv_ready, H + 1)
                nc.vector.tensor_tensor(
                    o_nat[:, half, 0:w * 8].rearrange("p (h d) -> p h d", d=w),
                    OB[:, 0:w * 8].rearrange("p (h d) -> p h d", d=w),
                    linv[:, p, hs].rearrange("p (h o) -> p h o", o=1).to_broadcast([P, 8, w]),
                    ALU.mult).then_inc(o_evac, 1)

            def residual(t, n):
                eng.wait_ge(wo_done, t * 2 + 2)
                if stage[0].first:
                    nc.vector.tensor_tensor(y_nat[:, n, :], YB[:, 0:C], bias_p[:, :], ALU.add).then_inc(y_free, 1)
                else:
                    nc.vector.tensor_tensor(xB[:, n + 1, 0:1], YB[:, P - 1:P], xA[:, n, P:P + 1], ALU.add)
                    nc.vector.tensor_tensor(xB[:, n, 1:P + 1], YB[:, 0:P], xA[:, n, 1:P + 1], ALU.add
                                            ).then_inc(y_free, 1)

            def copy_prev(t, n, p):
                at_least(eng, s_ready, (t - 1) * 8)
                at_least(eng, pv_done, (t - 1) * 8)
                nc.vector.tensor_scalar(kT[:, p, :, 0:WIN], kT[:, 1 - p, :, P:KEYS], follows[:, bass.ds(n, 1)], None, ALU.mult).then_inc(prev_ready, 1)
                nc.vector.tensor_copy(vprev[:, p, :], v[P - WIN:P, 1 - p, :]).then_inc(prev_ready, 1)

            def rotary(t, n, j, fresh=False):
                i = t - TILES
                Q, r, pj = i * 4 + j, j % 2, PJ[QK_AT[j] % 2]
                eng.wait_ge(pj_act, i * 6 + QK_AT[j] + 1)
                if not (fresh and j < 2):
                    eng.wait_ge(w_ready, Q - 1)
                heads3 = "p (h d) -> p h d"
                nc.vector.tensor_reduce(n2[:, r, :], sq[:, r, :].rearrange(heads3, d=D), AX.X, ALU.add
                                        ).then_inc(n2_ready, 1)
                k = 2 * (j % 2)
                nc.vector.tensor_tensor(
                    tc_[:, r, :].rearrange(heads3, d=D), pj[:, :].rearrange(heads3, d=D),
                    ropeL[:, k, n, :].rearrange("p (o d) -> p o d", o=1).to_broadcast([P, 8, D]), ALU.mult)
                for a in range(2):
                    lo, hi = a * (D // 2), (1 - a) * (D // 2)
                    last = nc.vector.tensor_tensor(
                        ts_[:, r, :].rearrange(heads3, d=D)[:, :, lo:lo + D // 2],
                        pj[:, :].rearrange(heads3, d=D)[:, :, hi:hi + D // 2],
                        ropeL[:, k + 1, n, lo:lo + D // 2].rearrange("p (o d) -> p o d", o=1
                                                                     ).to_broadcast([P, 8, D // 2]), ALU.mult)
                last.then_inc(pj_dve, 1)

            def qkv_first(t, p):
                eng.wait_ge(a_pj, t + 1)
                at_least(eng, tp_free, t)
                at_least(eng, pv_done, (t - 1) * 8)
                at_least(eng, prev_ready, t * 2)
                nc.vector.tensor_tensor(w_nat[:, 0, 0:2 * C], PJ[0][:, 0:2 * C], bias_a[:, 0:2 * C], ALU.add
                                        ).then_inc(a_qkv, 1)
                nc.vector.tensor_tensor(v[:, p, 0:C], PJ[0][:, 2 * C:3 * C], bias_a[:, 2 * C:3 * C], ALU.add
                                        ).then_inc(a_qkv, 1)

            stage = [FIRST]
            eng.wait_ge(x_loaded, 16 * SUPERS)
            norms(x_nat, 0)
            end(eng)
            begin(eng, 1)
            eng.wait_ge(c_loaded, CONSTS)
            copy_prev(0, 0, 0)
            qkv_first(0, 0)
            maxima(0, 0, 0)
            maxima(0, 0, 1)

            def tile_first(t, n, p, opening, closing):
                for c in range(CHUNKS):
                    if c == 1 and not opening:
                        heads_out(t - 1, 1 - p, 1)
                    if c == 5:
                        heads_out(t, p, 0)
                    if c not in LATE:
                        probs_T(t, c, opening)
                    if c < CHUNKS - 2:
                        maxima(t, p, c + 2)
                    elif not closing:
                        maxima(t + 1, 1 - p, c + 2 - CHUNKS)
                    if c in LATE:
                        probs_T(t, c, opening)
                    if c == 1 and not closing:
                        qkv_first(t + 1, 1 - p)
                    if c == 3 and not closing:
                        eng.wait_ge(tp_free, t + 1)
                        eng.wait_ge(a_qkv, t * 2 + 2)
                        copy_prev(t + 1, n + 1, 1 - p)
                    if c == 4 and not opening:
                        residual(t - 1, n - 1)

            def close(t, n, p):
                heads_out(t, p, 1)
                residual(t, n)
            tiles(eng, tile_first, close, 0)
            end(eng)
            begin(eng, 2)
            norms(y_nat, 1)
            eng.wait_ge(ln_step, 4)
            for n in range(TILES):
                last = nc.vector.tensor_tensor(x_nat[:, n, :], x_nat[:, n, :], ln_nat[:, n, :], ALU.add)
            last.then_inc(f_st, 1)
            eng.wait_ge(f_st, fst[0])
            fst[0] += 1
            norms(x_nat, 2)
            end(eng)
            stage[0] = LAYER
            base_st = fst[0] - 1
            with eng.Fori(0, DEPTH) as l:
                begin(eng, 3 + l * 2)
                t0 = TILES + l * TILES
                eng.wait_ge(rope_ready, l * 4 + 4)
                rotary(t0, 0, 0, True)
                rotary(t0, 0, 1, True)
                copy_prev(t0, 0, 0)
                rotary(t0, 0, 2, True)
                maxima(t0, 0, 0)
                maxima(t0, 0, 1)
                rotary(t0, 0, 3, True)

                def tile(t, n, p, opening, closing):
                    for c in range(CHUNKS):
                        if c == 1 and not opening:
                            heads_out(t - 1, 1 - p, 1)
                        if c == 5:
                            heads_out(t, p, 0)
                        if c not in LATE:
                            probs_T(t, c, opening)
                        if c < CHUNKS - 2:
                            maxima(t, p, c + 2)
                        elif not closing:
                            maxima(t + 1, 1 - p, c + 2 - CHUNKS)
                        if c in LATE:
                            probs_T(t, c, opening)
                        if c in ROTARY and not closing:
                            rotary(t + 1, n + 1, ROTARY[c])
                        if c == 3 and not closing:
                            eng.wait_ge(pj_act, (t - TILES) * 6 + 6)
                            eng.wait_ge(tp_free, TILES + (t - TILES) * 4 + 4)
                            copy_prev(t + 1, n + 1, 1 - p)
                        if c == 4 and not opening:
                            residual(t - 1, n - 1)
                tiles(eng, tile, close, t0)
                eng.wait_ge(y_free, t0 + TILES)
                nc.vector.memset(xB[:, PER_SEQ, 0:1], 0.0)
                end(eng)
                begin(eng, 4 + l * 2)
                eng.wait_ge(ffn_loaded, (l + 1) * 48)
                for s in range(SUPERS):
                    F = l * SUPERS + s
                    eng.wait_ge(f_t1, F + 1)
                    for j in range(SUPER):
                        last = nc.vector.bn_stats(stats[:, j, :], bank[0][:, j * C:(j + 1) * C])
                    eng.drain()
                    for j in range(SUPER):
                        last = nc.vector.bn_aggr(mv[:, j, :], stats[:, j, :])
                    last.then_inc(f_st, 1)
                    eng.wait_ge(f_st, F + 1 + base_st)
                    nc.vector.tensor_scalar(veps[:, 0:SUPER], mv[:, 0:SUPER, 1], EPS, None, ALU.add).then_inc(f_eps, 1)
                    eng.wait_ge(f_pow, F + 1)
                    if s:
                        eng.wait_ge(f_t2, F)
                    for j in range(SUPER):
                        last = nc.vector.tensor_scalar(xn[:, j, :], bank[0][:, j * C:(j + 1) * C], mv[:, j, 0:1],
                                                       rstd[:, j:j + 1], ALU.subtract, ALU.mult)
                    last.then_inc(f_xn, 1)
                    for i, (_, m) in enumerate(FF_CHUNKS):
                        k = F * 3 + i
                        r = (s * 3 + i) % 2
                        eng.wait_ge(f_act, k + 1)
                        eng.wait_ge(f_up, k + 1)
                        if s and i == 0:
                            eng.wait_ge(f_down, F)
                        nc.vector.scalar_tensor_tensor(hid[0:m, i, :], bank[4 + r][0:m, :], vec[0:m, 2 + i:3 + i],
                                                       gl[0:m, r, :], ALU.add, ALU.mult).then_inc(f_hid, 1)
                    eng.wait_ge(f_down, F + 1)
                    y4 = bank[6][:, :].rearrange("p (t q) -> p t q", t=SUPER)
                    t4 = slice(s * SUPER, (s + 1) * SUPER)
                    nc.vector.scalar_tensor_tensor(xA[:, s * SUPER + 1:(s + 1) * SUPER + 1, 0:1], y4[:, :, P - 1:P],
                                                   vec[:, 8:9], xB[:, t4, P:P + 1], ALU.add, ALU.add)
                    nc.vector.scalar_tensor_tensor(xA[:, t4, 1:P + 1], y4, vec[:, 8:9], xB[:, t4, 1:P + 1],
                                                   ALU.add, ALU.add).then_inc(f_out, 1)
                eng.wait_ge(f_out, (l + 1) * SUPERS)
                nc.vector.memset(xA[:, PER_SEQ, 0:1], 0.0)
                end(eng)
            begin(eng, LAST)
            eng.wait_ge(lnT_free, SUPERS)
            for n in range(TILES):
                last = nc.vector.bn_stats(stats[:, n, :], y_nat[:, n, :])
            last.then_inc(f_st, 1)
            at = base_st + DEPTH * SUPERS
            eng.wait_ge(f_st, at + 1)
            for n in range(TILES):
                last = nc.vector.bn_aggr(mv[:, n, :], stats[:, n, :])
            last.then_inc(f_st, 1)
            eng.wait_ge(f_st, at + 2)
            nc.vector.tensor_scalar(veps[:, :], mv[:, :, 1], EPS, None, ALU.add).then_inc(ln_step, 1)
            eng.wait_ge(ln_pow, 4)
            for n in range(TILES):
                last = nc.vector.tensor_scalar(ln_nat[:, n, :], y_nat[:, n, :], mv[:, n, 0:1], rstd[:, n:n + 1],
                                               ALU.subtract, ALU.mult)
            last.then_inc(f_st, 1)
            eng.wait_ge(f_st, at + 3)
            for s in range(SUPERS):
                t4 = slice(s * SUPER, (s + 1) * SUPER)
                nc.vector.tensor_tensor(x_nat[:, t4, :], x_nat[:, t4, :], ln_nat[:, t4, :], ALU.add).then_inc(out_ready, 1)

        @block.tensor
        def _(eng):
            def transposes(src, k):
                for s in range(SUPERS):
                    for j in range(SUPER):
                        last = nc.tensor.transpose(bank[s][:, j * P:(j + 1) * P], src(s * SUPER + j), idf[:, :])
                    last.then_inc(lnT_full, 1)

            def scores(t, n, p, c):
                st = stage[0]
                G, r = t * 8 + c, c % 2
                base, pair = st.heads(c)
                if c == 0:
                    eng.wait_ge(tp_free, t + 1 if st.first else TILES + (t - TILES) * 4 + 2)
                    eng.wait_ge(prev_ready, t * 2 + 2)
                if st.first:
                    eng.wait_ge(k_each, t * CHUNKS + c + 1)
                if c == 4 and not st.first:
                    eng.wait_ge(tp_free, TILES + (t - TILES) * 4 + 4)
                at_least(eng, p_ready, G - 1)
                nc.tensor.matmul(SB[r][:, 0:2 * KEYS], idb[:, :].bitcast(bf16),
                                 msk[:, n, :].bitcast(bf16).rearrange("p (o k) -> p o k", o=1).to_broadcast([P, 2, KEYS]),
                                 start=True, stop=False, skip_group_check=True)
                for h, (g, head) in enumerate(pair):
                    lhs, rhs = ((qT[:, p, 0, :], kEach[:, p, g, :]) if st.first else
                                (qT[base:base + D, p, g, :], kT[base:base + D, p, g, :]))
                    last = nc.tensor.matmul(SB[r][:, h * KEYS:(h + 1) * KEYS], lhs, rhs, start=False, stop=True,
                                            skip_group_check=True)
                last.then_inc(s_ready, 1)

            def transpose_probs(t, c, opening):
                G, r = t * 8 + c, c % 2
                eng.wait_ge(p_ready, G + 1)
                at_least(eng, pt_free, turn(t, c, opening))
                for h in range(2):
                    nc.tensor.transpose(PT[:, h * P:(h + 1) * P], prob[:, r, h, WIN:KEYS], idf[:, :])
                for h in range(2):
                    last = nc.tensor.transpose(PT[0:WIN, 2 * P + h * WIN:2 * P + (h + 1) * WIN],
                                               prob[0:WIN, r, h, 0:WIN], idf[0:WIN, 0:WIN])
                last.then_inc(pt_full, 1)

            def weigh_values(t, p, c, opening):
                st = stage[0]
                eng.wait_ge(pt_free, turn(t, c, opening) + 1)
                if c == 0:
                    at_least(eng, o_evac, t * 2)
                    if st.first:
                        eng.wait_ge(a_qkv, t * 2 + 2)
                    else:
                        eng.wait_ge(pj_act, (t - TILES) * 6 + V_AT[0] + 1)
                if c == 4:
                    eng.wait_ge(o_evac, t * 2 + 1)
                    if not st.first:
                        eng.wait_ge(pj_act, (t - TILES) * 6 + V_AT[1] + 1)
                r = c % 2
                for h, (g, head) in enumerate(st.heads(c)[1]):
                    a, vc = st.column(head), slice(head * st.K, (head + 1) * st.K)
                    nc.tensor.matmul(OB[:, a:a + st.K], pT[:, r, h, :], v[:, p, vc], start=True, stop=False,
                                     skip_group_check=True)
                    last = nc.tensor.matmul(OB[0:WIN, a:a + st.K], pTprev[:, r, h, :], vprev[:, p, vc],
                                            start=False, stop=True, skip_group_check=True)
                last.then_inc(pv_done, 1)

            def project(t, p, x, fresh=False):
                i = t - TILES
                if x == 0:
                    eng.wait_ge(xs_ready, t * 2 + 2)
                if not (fresh and x < 2):
                    eng.wait_ge(pj_act, i * 6 + x - 1)
                    if x in (0, 2, 3, 4):
                        eng.wait_ge(pj_dve, i * 4 + {0: 0, 2: 1, 3: 2, 4: 3}[x])
                col = [0, INNER, HB, 2 * INNER, INNER + HB, 2 * INNER + HB][x]
                nc.tensor.matmul(PJ[x % 2][:, :], xs[:, p, :], wqkv[:, col:col + HB], start=True, stop=True
                                 ).then_inc(pj_ready, 1)

            def transpose_heads(t, j):
                Q = (t - TILES) * 4 + j
                eng.wait_ge(w_ready, Q + 1)
                eng.wait_ge(tp_free, TILES + Q)
                for i in range(4):
                    last = nc.tensor.transpose(TP[:, i * P:(i + 1) * P], w_nat[:, j % 2, i * P:(i + 1) * P], idf[:, :])
                last.then_inc(tp_full, 1)

            def project_first(t, p):
                eng.wait_ge(xs_ready, t * 2 + 2)
                at_least(eng, a_qkv, t * 2)
                nc.tensor.matmul(PJ[0][:, 0:3 * C], xs[:, p, :], wa[:, :], start=True, stop=True).then_inc(a_pj, 1)

            def transpose_first(t):
                eng.wait_ge(a_qkv, t * 2 + 1)
                at_least(eng, tp_free, t)
                for i in range(2):
                    last = nc.tensor.transpose(TP[:, i * P:(i + 1) * P], w_nat[:, 0, i * P:(i + 1) * P], idf[:, :])
                last.then_inc(tp_full, 1)

            def transpose_out(t, half, closing):
                eng.wait_ge(o_evac, t * 2 + half + 1)
                eng.wait_ge(pt_free, out_turn(t, half, closing))
                for i in range(1 if stage[0].first else 4):
                    last = nc.tensor.transpose(PT[:, i * P:(i + 1) * P], o_nat[:, half, i * P:(i + 1) * P], idf[:, :])
                last.then_inc(pt_full, 1)

            def project_out(t, half, closing):
                eng.wait_ge(pt_free, out_turn(t, half, closing) + 1)
                if half == 0:
                    at_least(eng, y_free, t)
                if stage[0].first:
                    nc.tensor.matmul(YB[:, 0:C], oT[0:C // 2, half, 0:P], wp[:, half, :], start=half == 0,
                                     stop=half == 1).then_inc(wo_done, 1)
                    return
                for i in range(4):
                    last = nc.tensor.matmul(YB[:, 0:P], wo[:, 4 * half + i, :], oT[:, half, i * P:(i + 1) * P],
                                            start=half == 0 and i == 0, stop=half == 1 and i == 3)
                last.then_inc(wo_done, 1)

            def tile(t, n, p, opening, closing):
                for c in range(CHUNKS):
                    if c not in LATE:
                        transpose_probs(t, c, opening)
                    if c < CHUNKS - 2:
                        scores(t, n, p, c + 2)
                    elif not closing:
                        scores(t + 1, n + 1, 1 - p, c + 2 - CHUNKS)
                    if stage[0].first:
                        if not closing:
                            if c == 0:
                                project_first(t + 1, 1 - p)
                            if c == 2:
                                transpose_first(t + 1)
                    else:
                        if not closing and c in PROJECT:
                            project(t + 1, 1 - p, PROJECT[c])
                    if c:
                        weigh_values(t, p, c - 1, opening)
                    elif not opening:
                        weigh_values(t - 1, 1 - p, CHUNKS - 1, False)
                    if c in LATE:
                        transpose_probs(t, c, opening)
                    if not stage[0].first:
                        if c == 0 and opening:
                            transpose_heads(t, 2)
                        if c == 1:
                            transpose_heads(t, 3)
                        if not closing and c in HEADS_T:
                            transpose_heads(t + 1, HEADS_T[c])
                    if not opening:
                        if c == 2:
                            transpose_out(t - 1, 1, False)
                        if c == 3:
                            project_out(t - 1, 1, False)
                    if c == 6:
                        transpose_out(t, 0, False)
                    if c == 7:
                        project_out(t, 0, False)

            def close(t, n, p):
                weigh_values(t, p, CHUNKS - 1, False)
                transpose_out(t, 1, True)
                project_out(t, 1, True)

            stage = [FIRST]
            eng.wait_ge(c_loaded, CONSTS)
            eng.wait_ge(ln_step, 2)
            transposes(lambda n: ln_nat[:, n, :], 0)
            end(eng)
            begin(eng, 1)
            project_first(0, 0)
            transpose_first(0)
            scores(0, 0, 0, 0)
            scores(0, 0, 0, 1)

            tiles(eng, tile, close, 0)
            end(eng)
            begin(eng, 2)
            eng.wait_ge(ln_step, 6)
            transposes(lambda n: ln_nat[:, n, :], 1)
            end(eng)
            stage[0] = LAYER
            with eng.Fori(0, DEPTH) as l:
                begin(eng, 3 + l * 2)
                eng.wait_ge(att_loaded, (l + 1) * 48)
                t0 = TILES + l * TILES
                project(t0, 0, 0, True)
                project(t0, 0, 1, True)
                project(t0, 0, 2, True)
                project(t0, 0, 3, True)
                transpose_heads(t0, 0)
                transpose_heads(t0, 1)
                scores(t0, 0, 0, 0)
                scores(t0, 0, 0, 1)
                project(t0, 0, 4, True)
                project(t0, 0, 5, True)
                tiles(eng, tile, close, t0)
                end(eng)
                begin(eng, 4 + l * 2)
                eng.wait_ge(ffn_loaded, (l + 1) * 48)
                for s in range(SUPERS):
                    F, r2 = l * SUPERS + s, s % 2
                    eng.wait_ge(f_x, F * 2 + 2)
                    if s:
                        eng.wait_ge(f_xn, F)
                    for j in range(SUPER):
                        last = nc.tensor.transpose(bank[0][:, j * C:(j + 1) * C], xf[:, r2, j, :], idf[:, :])
                    last.then_inc(f_t1, 1)
                    eng.wait_ge(f_xn, F + 1)
                    for j in range(SUPER):
                        last = nc.tensor.transpose(bank[1][:, j * P:(j + 1) * P], xn[:, j, :], idf[:, :])
                    last.then_inc(f_t2, 1)
                    eng.wait_ge(f_xnT, F + 1)
                    for i, (a, m) in enumerate(FF_CHUNKS):
                        k = F * 3 + i
                        r = (s * 3 + i) % 2
                        if s * 3 + i >= 2:
                            eng.wait_ge(f_hid, k - 1)
                        nc.tensor.matmul(bank[2 + r][0:m, :], w1[:, FF + a:FF + a + m], xnT[:, :], start=True, stop=True
                                         ).then_inc(f_gate, 1)
                        nc.tensor.matmul(bank[4 + r][0:m, :], w1[:, a:a + m], xnT[:, :], start=True, stop=True
                                         ).then_inc(f_up, 1)
                    eng.wait_ge(f_hid, F * 3 + 3)
                    if s:
                        eng.wait_ge(f_out, F)
                    for i, (_, m) in enumerate(FF_CHUNKS):
                        last = nc.tensor.matmul(bank[6][:, :], w2[0:m, i, :], hid[0:m, i, :], start=i == 0, stop=i == 2)
                    last.then_inc(f_down, 1)
                end(eng)
            begin(eng, LAST)
            transposes(lambda n: xA[:, n, 1:P + 1], 2)


def ropeS(scl, k, P, B):
    return scl[:, k, :].rearrange("p (o d) -> p o d", o=1).to_broadcast([P, B * 8, 64])


def _constants():
    import numpy as np
    f = np.float32
    half = np.arange(0, D, 2, dtype=f)
    inv_freq = (f(1.0) / f(10000.0) ** (half / f(D))).astype(f)
    t = np.arange(N, dtype=f)
    freqs = t[:, None] * inv_freq[None, :]
    freqs = np.concatenate([freqs, freqs], -1)
    base = (half + f(0.4 * D)) / f(1.4 * D)
    scale = base[None, :] ** ((t - f(N // 2)) / f(WIN // 2))[:, None]
    scale = np.concatenate([scale, scale], -1).astype(f)
    cos, sin = np.cos(freqs), np.sin(freqs)
    sign = np.concatenate([-np.ones(D // 2, f), np.ones(D // 2, f)])
    inv = f(1.0) / scale
    tabs = np.stack([cos * scale, sin * sign * scale, cos * inv * f(8), sin * sign * inv * f(8)])
    rope = tabs.reshape(4, PER_SEQ, P, D).transpose(2, 0, 1, 3).astype(f)
    i = np.arange(P)[:, None]
    j = np.arange(KEYS)[None, :] - WIN
    ok = (j <= i) & (j >= i - WIN)
    tile = np.arange(TILES)[:, None, None] % PER_SEQ
    ok = ok[None] & ((j[None] >= 0) | (tile > 0))
    mask = np.where(ok, 0.0, -1e30).transpose(1, 0, 2).astype(f)
    eye = np.eye(P, dtype=f)
    
    def bf16_bits(a):
        return (np.ascontiguousarray(a).view(np.uint32) >> 16).astype(np.uint16)
    return np.ascontiguousarray(rope), eye, bf16_bits(eye), bf16_bits(mask)


def kernel(L0_attn_x, L0_attn_W_attn, L0_attn_b_attn, L0_attn_W_proj, L0_attn_b_proj, L0_ffn_Wqkv, L0_ffn_q_scale,
           L0_ffn_k_scale, L0_ffn_Wo, L0_ffn_ln_g, L0_ffn_ln_b, L0_ffn_W1, L0_ffn_b1, L0_ffn_W2, L0_ffn_b2):
    import numpy as np
    import concourse.bacc as bacc
    from concourse.bass_utils import run_bass_kernel_spmd

    A = np.ascontiguousarray
    rope, eye, eyeb, mask = _constants()

    def swap(s):
        return np.concatenate([s[:, D // 2:], s[:, :D // 2]], -1)
    qs, ks = np.asarray(L0_ffn_q_scale), np.asarray(L0_ffn_k_scale)
    scales = np.stack([qs, swap(qs), ks, swap(ks)], 1)
    scales = A(np.broadcast_to(scales[:, None], (DEPTH, P, 4, D)))
    par = np.zeros((DEPTH, P, PAR), np.float32)
    b1 = np.asarray(L0_ffn_b1)
    par[:, :, 0], par[:, :, 1], par[:, :, 8] = np.asarray(L0_ffn_ln_g), np.asarray(L0_ffn_ln_b), np.asarray(L0_ffn_b2)
    for i, (a, m) in enumerate(FF_CHUNKS):
        par[:, :m, 2 + i] = b1[:, a:a + m]
        par[:, :m, 5 + i] = b1[:, FF + a:FF + a + m]
    w2 = np.zeros((DEPTH, 3 * P, C), np.float32)
    w2[:, :FF] = np.asarray(L0_ffn_W2)
    ins = {
        "x": A(np.asarray(L0_attn_x).reshape(B * N, C)), "w_attn": A(L0_attn_W_attn),
        "b_attn": A(np.broadcast_to(np.asarray(L0_attn_b_attn), (P, 3 * C))), "w_proj": A(L0_attn_W_proj),
        "b_proj": A(np.broadcast_to(np.asarray(L0_attn_b_proj), (P, C))), "w_qkv": A(L0_ffn_Wqkv),
        "w_o": A(L0_ffn_Wo), "scales": scales, "w_1": A(L0_ffn_W1), "w_2": w2, "vectors": par, "rope": rope,
        "identity": eye, "identity_bf16": eyeb, "mask": mask, "select": np.repeat(np.eye(HEADS, dtype=np.float32), DA, 0),
    }
    nc = bacc.Bacc("TRN2", target_bir_lowering=False, num_devices=1)
    aps = [nc.dram_tensor(k, a.shape, mybir.dt.from_np(a.dtype), kind="ExternalInput").ap() for k, a in ins.items()]
    out = nc.dram_tensor("out", (B * N, C), mybir.dt.float32, kind="ExternalOutput").ap()
    build(nc, *aps, out)
    r = run_bass_kernel_spmd(nc, [ins], core_ids=[0])
    return r.results[0]["out"].reshape(B, N, C)
```

```python
import concourse.bass as bass
from concourse import mybir
from contextlib import ExitStack

B, N, C, P = 2, 1024, 128, 128
TILES = B * N // P
PER_SEQ = N // P
DEPTH, HEADS, WIN = 6, 16, 32
D = 64
DA = C // HEADS
INNER = HEADS * D
FF = int(C * 4 * 2 / 3)
KEYS = WIN + P
HALF = P // 2
FF_CHUNKS = [(0, 128), (128, 128), (256, FF - 256)]
CHUNKS = HEADS // 2
SUPER = 4
SUPERS = TILES // SUPER
HB = 8 * D
PAR = 9
EPS = 1e-5


class Stage:

    def __init__(self, first):
        self.first = first
        self.K = DA if first else D
        self.half = 8 * self.K

    def heads(self, c):
        if self.first:
            return 0, [(2 * c, 2 * c), (2 * c + 1, 2 * c + 1)]
        return 64 * (c % 2), [(g, 2 * g + c % 2) for g in (2 * (c // 2), 2 * (c // 2) + 1)]

    def column(self, head):
        return (head % 8) * self.K


def turn(t, c, opening):
    return t * 10 + (c - (0 if opening else 1) if c < 3 else c if c < 7 else 8)


def out_turn(t, half, closing):
    return t * 10 + (7 if half == 0 else 9 if closing else 12)


QK_AT, V_AT = [0, 1, 2, 4], [3, 5]
PROJECT = {0: 0, 1: 1, 3: 2, 4: 3, 5: 4, 7: 5}
SQUARE = {0: 0, 1: 1, 3: 2, 5: 3}
ROTARY = {1: 0, 2: 1, 3: 2, 6: 3}
VALUES = {4: 0, 7: 1}
LATE = (3, 7)
HEADS_T = {3: 0, 5: 1, 7: 2}
HEADS_FIRST = (1, 5)
COPY_PREV, RESIDUAL = 4, 4
ACT_COPIES = (0, 1)

FIRST, LAYER = Stage(True), Stage(False)


def build(nc, x, Wa, ba, Wp, bp, Wqkv, Wo, scales, W1, W2, par, rope, ident, identb, mask, select, out):
    f32, f32r, bf16 = mybir.dt.float32, mybir.dt.float32r, mybir.dt.bfloat16
    ALU, ACT, AX = mybir.AluOpType, mybir.ActivationFunctionType, mybir.AxisListType
    ctx = ExitStack()
    with ctx:
        def sb(name, shape, dt=f32):
            return ctx.enter_context(nc.sbuf_tensor(name, shape, dt))

        def sem(name):
            return ctx.enter_context(nc.semaphore(name))

        x_nat = sb("x_nat", [P, TILES, C])
        nat2 = sb("nat2", [P, 2, TILES, C])
        y_nat, ln_nat = nat2[:, 0], nat2[:, 1]
        xA = sb("xA", [C, TILES + 1, P + 1])
        xB = sb("xB", [C, TILES + 1, P + 1])
        wa = sb("wa", [C, 3 * C])
        wp = sb("wp", [C // 2, 2, C])
        bias_a = sb("bias_a", [P, 3 * C])
        bias_p = sb("bias_p", [P, C])
        w_hi = sb("w_hi", [C, 3 * INNER], f32r)
        w_lo = sb("w_lo", [C, 3 * INNER], f32r)
        wo = sb("wo", [P, CHUNKS, C])
        w1 = sb("w1", [C, 2 * FF])
        w2 = sb("w2", [P, 3, C])
        vec = sb("vec", [P, PAR])
        scl = sb("scl", [P, 4, D])
        rope0 = sb("rope0", [P, 4, PER_SEQ, D])
        ropeL = sb("ropeL", [P, 4, TILES, D])
        idf = sb("idf", [P, P])
        idb = sb("idb", [P, P], mybir.dt.uint16)
        sel = sb("sel", [P, HEADS])
        wqkv = nat2[:, :, :, :].rearrange("p a t c -> p (a t c)")[:, 0:3 * INNER]
        shared = sb("shared", [P, 2 * HEADS * KEYS])
        kEach = shared[:, :].rearrange("p (a h k) -> p a h k", a=2, h=HEADS)
        wqkv0 = shared[:, 0:3 * INNER]
        msk = sb("msk", [P, TILES, P], mybir.dt.uint16)
        follows = sb("follows", [P, TILES])
        half_neg = sb("half_neg", [P, TILES])
        xs0 = sb("xs0", [C, 2, P])
        xs = sb("xs", [C, 2, P], f32r)
        xs_lo = sb("xs_lo", [C, 2, P], f32r)
        sq = sb("sq", [P, 2, HB])
        n2 = sb("n2", [P, 2, 8])
        n2c = sb("n2c", [P, 2, 8])
        rn = sb("rn", [P, 2, 8])
        tc_ = sb("tc_", [P, 2, HB])
        ts_ = sb("ts_", [P, 2, HB])
        tsum = sb("tsum", [P, 2, HB])
        w_nat = sb("w_nat", [P, 2, HB])
        qT = sb("qT", [P, 2, 8, P])
        kT = sb("kT", [P, 2, 8, KEYS])
        v = sb("v", [P, 2, INNER])
        vlow = sb("vlow", [P, 2, INNER])
        nmax = sb("nmax", [P, 2, HEADS])
        prob = sb("prob", [P, 2, 2, P])
        lsum = sb("lsum", [P, 2, HEADS])
        linv = sb("linv", [P, 2, HEADS])
        pT = sb("pT", [P, 2, 2, P])
        o_nat = sb("o_nat", [P, 2, HB])
        oT = sb("oT", [P, 2, HB])
        used = 2 * 3 * SUPER * P
        xf = shared[:, used:used + 2 * SUPER * P].rearrange("p (a t q) -> p a t q", a=2, t=SUPER)
        used += 2 * SUPER * P
        xn = sb("xn", [P, SUPER, C])
        xnT = sb("xnT", [C, 2, SUPER * P])
        gl = shared[:, used:used + 2 * SUPER * P].rearrange("p (a q) -> p a q", a=2)
        hid = shared[:, 0:2 * 3 * SUPER * P].rearrange("p (a i q) -> p a i q", a=2, i=3)
        stats = sb("stats", [P, TILES, 6])
        mv = sb("mv", [P, TILES, 2])
        veps = sb("veps", [P, TILES])
        rstd = sb("rstd", [P, TILES])

        bank = [ctx.enter_context(nc.psum_tensor(f"bank{i}", [P, 512], f32)) for i in range(8)]
        PJ, SB, PT, OB, TP, YB = bank[0:2], bank[2:4], bank[4], bank[5], bank[6], bank[7]

        phase = sem("phase")
        x_loaded, c_loaded = sem("x_loaded"), sem("c_loaded")
        scl_loaded, qkv_loaded, wo_loaded = sem("scl_loaded"), sem("qkv_loaded"), sem("wo_loaded")
        ffn_loaded = sem("ffn_loaded")
        edge = sem("edge")
        init_done = sem("init_done")
        rope_ready = sem("rope_ready")
        xs_ready = sem("xs_ready")
        xs_rest = sem("xs_rest")
        w_split, w_rest = sem("w_split"), sem("w_rest")
        pj_ready = sem("pj_ready")
        pj_act = sem("pj_act")
        pj_dve = sem("pj_dve")
        n2_ready = sem("n2_ready")
        n2c_ready = sem("n2c_ready")
        pool_step = sem("pool_step")
        w_ready = sem("w_ready")
        tp_full, tp_free = sem("tp_full"), sem("tp_free")
        prev_ready = sem("prev_ready")
        s_ready = sem("s_ready")
        max_ready = sem("max_ready")
        p_ready = sem("p_ready")
        pt_full, pt_free = sem("pt_full"), sem("pt_free")
        pv_done = sem("pv_done")
        linv_ready = sem("linv_ready")
        o_evac = sem("o_evac")
        wo_done = sem("wo_done")
        y_free = sem("y_free")
        a_qkv = sem("a_qkv")
        k_each = sem("k_each")
        a_pj = sem("a_pj")
        ln_step, ln_pow = sem("ln_step"), sem("ln_pow")
        lnT_full, lnT_free = sem("lnT_full"), sem("lnT_free")
        f_x, f_t1, f_st, f_eps, f_pow, f_xn, f_t2, f_xnT = (sem(n) for n in (
            "f_x", "f_t1", "f_st", "f_eps", "f_pow", "f_xn", "f_t2", "f_xnT"))
        f_gate, f_act, f_up, f_hid, f_down, f_out = (sem(n) for n in (
            "f_gate", "f_act", "f_up", "f_hid", "f_down", "f_out"))
        out_ready, out_stored = sem("out_ready"), sem("out_stored")

        CONSTS = 16 * 9

        def at_least(eng, s, value):
            if not (isinstance(value, int) and value <= 0):
                eng.wait_ge(s, value)

        def begin(eng, k):
            at_least(eng, phase, 4 * k)

        def end(eng):
            eng.drain().then_inc(phase, 1)

        T1, T2, GATE, UP, DOWN = bank[0:2], bank[6], (bank[2], bank[4]), (bank[3], bank[5]), bank[7]

        def tiles(eng, tile, close, base):
            tile(base, 0, 0, True, False)
            tile(base + 1, 1, 1, False, False)
            with eng.Fori(1, TILES // 2 - 1) as i:
                tile(base + i * 2, i * 2, 0, False, False)
                tile(base + i * 2 + 1, i * 2 + 1, 1, False, False)
            tile(base + TILES - 2, TILES - 2, 0, False, False)
            tile(base + TILES - 1, TILES - 1, 1, False, True)
            close(base + TILES - 1, TILES - 1, 1)

        def probs_T(eng, t, c, opening, copy):
            G, r = t * 8 + c, c % 2
            eng.wait_ge(pt_full, turn(t, c, opening) + 1)
            at_least(eng, pv_done, G - 1)
            copy(pT[:, r, :, :], PT[:, 0:2 * P].rearrange("p (h q) -> p h q", h=2)).then_inc(pt_free, 1)

        block = ctx.enter_context(nc.Block())

        @block.sync
        def _(eng):
            for s in range(SUPERS):
                eng.dma_start(x_nat[:, s * SUPER:(s + 1) * SUPER, :],
                              x[s * SUPER * P:(s + 1) * SUPER * P, :].rearrange("(t p) c -> p t c", p=P)
                              ).then_inc(x_loaded, 16)
            for dst, src in ((idf[:, :], ident), (idb[:, :], identb), (wa[:, :], Wa),
                             (wp[:, :, :], Wp.rearrange("(h p) c -> p h c", h=2)),
                             (bias_a[:, :], ba), (bias_p[:, :], bp), (msk[:, :, :], mask),
                             (rope0[:, :, :, :], rope), (sel[:, :], select)):
                eng.dma_start(dst, src).then_inc(c_loaded, 16)
            for l in range(DEPTH):
                if l:
                    eng.wait_ge(rope_ready, 4 * l)
                eng.dma_start(scl[:, :, :], scales[l, :, :, :]).then_inc(scl_loaded, 16)
                if l == 0:
                    eng.wait_ge(phase, 4 * 2)
                if l == 1:
                    eng.wait_ge(phase, 4 * 3)
                if l > 1:
                    eng.wait_ge(w_rest, 3 * l)
                eng.dma_start((wqkv if l else wqkv0)[:, :], Wqkv[l, :, :]).then_inc(qkv_loaded, 16)
                if l:
                    eng.wait_ge(wo_done, 2 * TILES * (l + 1))
                eng.dma_start(wo[:, :, :], Wo[l, :, :].rearrange("(i p) c -> p i c", p=P)).then_inc(wo_loaded, 16)
                if l:
                    eng.wait_ge(f_out, SUPERS * l)
                eng.dma_start(w1[:, :], W1[l, :, :]).then_inc(ffn_loaded, 16)
                eng.dma_start(w2[:, :, :], W2[l, :, :].rearrange("(i p) c -> p i c", p=P)).then_inc(ffn_loaded, 16)
                eng.dma_start(vec[:, :], par[l, :, :]).then_inc(ffn_loaded, 16)
            for s in range(SUPERS):
                eng.wait_ge(out_ready, s + 1)
                eng.dma_start(out[s * SUPER * P:(s + 1) * SUPER * P, :].rearrange("(t p) c -> p t c", p=P),
                              x_nat[:, s * SUPER:(s + 1) * SUPER, :]).then_inc(out_stored, 16)
            eng.wait_ge(out_stored, 16 * SUPERS)

        @block.gpsimd
        def _(eng):
            nc.gpsimd.memset(half_neg[:, :], -0.5).then_inc(init_done, 1)
            nc.gpsimd.memset(w_nat[:, :, :], 0.0).then_inc(init_done, 1)
            nc.gpsimd.memset(kT[:, :, :, :], 0.0).then_inc(init_done, 1)
            nc.gpsimd.memset(v[:, :, :], 0.0).then_inc(init_done, 1)
            nc.gpsimd.memset(xA[:, :, :], 0.0).then_inc(init_done, 1)
            nc.gpsimd.memset(xB[:, :, :], 0.0).then_inc(init_done, 1)
            nc.gpsimd.memset(o_nat[:, :, 0:P], 0.0).then_inc(init_done, 1)
            nc.gpsimd.memset(follows[:, :], 1.0).then_inc(init_done, 1)
            eng.wait_ge(init_done, 8)
            nc.gpsimd.memset(follows[:, 0:TILES:PER_SEQ], 0.0).then_inc(init_done, 1)
            eng.wait_ge(init_done, 9)

            def pow_rstd(k):
                eng.wait_ge(ln_step, 2 * k + 1)
                nc.gpsimd.tensor_tensor(rstd[:, :], veps[:, :], half_neg[:, :], ALU.pow).then_inc(ln_pow, 1)

            def rotate(q_idx):
                for j in range(4):
                    r, Q = j % 2, q_idx + j
                    eng.wait_ge(n2c_ready, Q + 1)
                    nc.gpsimd.tensor_tensor(rn[:, r, :], n2c[:, r, :], half_neg[:, 0:8], ALU.pow).then_inc(pool_step, 1)
                    eng.wait_ge(pj_dve, Q + 1)
                    nc.gpsimd.tensor_tensor(tsum[:, r, :], tc_[:, r, :], ts_[:, r, :], ALU.add).then_inc(pool_step, 1)
                    eng.wait_ge(pool_step, 2 * Q + 2)
                    at_least(eng, tp_free, TILES + Q - 1)
                    nc.gpsimd.tensor_tensor(
                        w_nat[:, r, :].rearrange("p (h d) -> p h d", d=D), tsum[:, r, :].rearrange("p (h d) -> p h d", d=D),
                        rn[:, r, :].rearrange("p (h o) -> p h o", o=1).to_broadcast([P, 8, D]), ALU.mult).then_inc(w_ready, 1)

            pow_rstd(0)
            end(eng)
            begin(eng, 1)

            def split_keys(t, p):
                for c in range(CHUNKS):
                    if c == 0:
                        eng.wait_ge(tp_free, t + 1)
                        eng.wait_ge(prev_ready, t * 2 + 2)
                    nc.gpsimd.tensor_tensor(
                        kEach[:, p, 2 * c:2 * c + 2, :],
                        kT[:, p, 0, :].rearrange("p (o k) -> p o k", o=1).to_broadcast([P, 2, KEYS]),
                        sel[:, 2 * c:2 * c + 2].rearrange("p (h o) -> p h o", o=1).to_broadcast([P, 2, KEYS]),
                        ALU.mult).then_inc(k_each, 1)
            split_keys(0, 0)
            split_keys(1, 1)
            with eng.Fori(1, TILES // 2) as i:
                split_keys(i * 2, 0)
                split_keys(i * 2 + 1, 1)

            def tables(l):
                eng.wait_ge(scl_loaded, (l + 1) * 16)
                for k in range(4):
                    nc.gpsimd.tensor_tensor(
                        ropeL[:, k, :, :].rearrange("p (b t) d -> p b (t d)", b=B),
                        rope0[:, k, :, :].rearrange("p (o t) d -> p o (t d)", o=1).to_broadcast([P, B, PER_SEQ * D]),
                        scl[:, k, :].rearrange("p (o d) -> p o d", o=1).to_broadcast([P, TILES, D]),
                        ALU.mult).then_inc(rope_ready, 1)
            def rest(l, k, first=False):
                eng.wait_ge(w_split, l * 3 + k + 1)
                cols = slice(k * INNER, (k + 1) * INNER)
                nc.gpsimd.tensor_tensor(w_lo[:, cols], (wqkv0 if first else wqkv)[:, cols], w_hi[:, cols].bitcast(f32),
                                        ALU.subtract).then_inc(w_rest, 1)
            eng.wait_ge(c_loaded, CONSTS)
            tables(0)
            end(eng)
            begin(eng, 2)
            pow_rstd(1)
            rest(0, 0, True)
            rest(0, 1, True)
            pow_rstd(2)
            rest(0, 2, True)
            end(eng)
            begin(eng, 3)
            rotate(0)

            def layer(l, last):
                with eng.Fori(1, TILES) as n:
                    rotate((l * TILES + n) * 4)
                for s in range(SUPERS):
                    F = l * SUPERS + s
                    eng.wait_ge(f_eps, F + 1)
                    nc.gpsimd.tensor_tensor(rstd[:, 0:SUPER], veps[:, 0:SUPER], half_neg[:, 0:SUPER], ALU.pow
                                            ).then_inc(f_pow, 1)
                    if not last and s in (1, 2):
                        for k in range(s - 1, 2 * s - 1):
                            rest(l + 1, k)
                if not last:
                    tables(l + 1)
                    rotate((l + 1) * TILES * 4)
            with eng.Fori(0, DEPTH - 1) as l:
                layer(l, False)
            layer(DEPTH - 1, True)
            pow_rstd(3)

        @block.scalar
        def _(eng):
            def lnT(k):
                for s in range(SUPERS):
                    K = k * SUPERS + s
                    eng.wait_ge(lnT_full, K + 1)
                    src = bank[s][:, :].rearrange("p (t q) -> p t q", t=SUPER)
                    tl = slice(s * SUPER, (s + 1) * SUPER)
                    nc.scalar.activation(xA[:, tl, 1:P + 1], src, ACT.Copy)
                    for j in range(SUPER):
                        n = s * SUPER + j + 1
                        if n % PER_SEQ:
                            nc.scalar.activation(xA[:, n, 0:1], src[:, j, P - 1:P], ACT.Copy)

            def copy_input(n, p, shift):
                lo = C // 2
                a, dst = (0, xs) if shift else (1, xs0)
                nc.scalar.activation(dst[0:lo, p, :], xA[0:lo, n, 1:P + 1], ACT.Copy).then_inc(xs_ready, 1)
                nc.scalar.activation(dst[lo:C, p, :], xA[lo:C, n, a:P + a], ACT.Copy).then_inc(xs_ready, 1)

            def split(l, k, first=False):
                eng.wait_ge(qkv_loaded, (l + 1) * 16)
                if not first:
                    eng.wait_ge(pj_ready, l * (6 * TILES))
                cols = slice(k * INNER, (k + 1) * INNER)
                nc.scalar.activation(w_hi[:, cols], (wqkv0 if first else wqkv)[:, cols], ACT.Copy).then_inc(w_split, 1)

            def shifted(l, s):
                lo, tl = C // 2, slice(s * SUPER, (s + 1) * SUPER)
                eng.wait_ge(y_free, (l + 1) * TILES + (s + 1) * SUPER)
                if s >= 2:
                    eng.wait_ge(edge, l + 1)
                    eng.wait_ge(f_t1, l * SUPERS + s - 1)
                nc.scalar.activation(xf[0:lo, s % 2, :, :], xB[0:lo, tl, 1:P + 1], ACT.Copy).then_inc(f_x, 1)
                nc.scalar.activation(xf[lo:C, s % 2, :, :], xB[lo:C, tl, 0:P], ACT.Copy).then_inc(f_x, 1)

            def exps(t, p, c, opening):
                st = stage[0]
                G, r = t * 8 + c, c % 2
                eng.wait_ge(max_ready, G + 1)
                at_least(eng, pt_full, (turn(t, c - 2, opening) if c >= 2 else turn(t - 1, c + 6, False)) + 1)
                for h, (g, head) in enumerate(st.heads(c)[1]):
                    last = nc.scalar.activation(
                        prob[:, r, h, :], SB[r][:, h * P:(h + 1) * P], ACT.Exp,
                        bias=nmax[:, p, 2 * c + h:2 * c + h + 1], accum_out=lsum[:, p, head:head + 1])
                last.then_inc(p_ready, 1)

            def square(t, j, fresh=False):
                J, Q = (t - TILES) * 6 + QK_AT[j], (t - TILES) * 4 + j
                eng.wait_ge(pj_ready, J + 1)
                if not (fresh and j < 2):
                    eng.wait_ge(n2_ready, Q - 1)
                nc.scalar.activation(sq[:, j % 2, :], PJ[QK_AT[j] % 2][:, :], ACT.Square).then_inc(pj_act, 1)

            def values(t, p, j):
                J = (t - TILES) * 6 + V_AT[j]
                eng.wait_ge(pj_ready, J + 1)
                eng.wait_ge(pv_done, (t - 1) * 8)
                eng.wait_ge(prev_ready, t * 2)
                nc.scalar.activation(vlow[0:P - WIN, p, j * HB:(j + 1) * HB], PJ[V_AT[j] % 2][0:P - WIN, :], ACT.Copy)
                nc.scalar.activation(v[:, p, j * HB:(j + 1) * HB], PJ[V_AT[j] % 2][:, :], ACT.Copy).then_inc(pj_act, 1)

            def heads_out_T(t, half, closing):
                eng.wait_ge(pt_full, out_turn(t, half, closing) + 1)
                at_least(eng, wo_done, (t - 1) * 2 + half + 1)
                rows, cols = (C // 2, P) if stage[0].first else (P, HB)
                nc.scalar.activation(oT[0:rows, half, 0:cols], PT[0:rows, 0:cols], ACT.Copy).then_inc(pt_free, 1)

            def heads_T(t, p, j):
                Q = TILES + (t - TILES) * 4 + j
                eng.wait_ge(tp_full, Q + 1)
                eng.wait_ge(s_ready, (t - 1) * 8)
                eng.wait_ge(prev_ready, t * 2)
                src = TP[:, :].rearrange("p (g q) -> p g q", g=4)
                g0 = 4 * (j // 2)
                dst = qT[:, p, g0:g0 + 4, :] if j % 2 == 0 else kT[:, p, g0:g0 + 4, WIN:KEYS]
                nc.scalar.activation(dst, src, ACT.Copy).then_inc(tp_free, 1)

            def heads_T_first(t, p):
                at_least(eng, s_ready, (t - 1) * 8)
                at_least(eng, prev_ready, t * 2)
                eng.wait_ge(tp_full, t + 1)
                nc.scalar.activation(qT[:, p, 0, :], TP[:, 0:P], ACT.Copy, scale=DA ** -0.5)
                nc.scalar.activation(kT[:, p, 0, WIN:KEYS], TP[:, P:2 * P], ACT.Copy).then_inc(tp_free, 1)

            stage = [FIRST]
            eng.wait_ge(init_done, 9)
            lnT(0)
            end(eng)
            begin(eng, 1)
            copy_input(0, 0, False)
            heads_T_first(0, 0)
            exps(0, 0, 0, True)

            def tile_first(t, n, p, opening, closing):
                if not closing:
                    copy_input(n + 1, 1 - p, False)
                for c in range(CHUNKS):
                    if c in ACT_COPIES:
                        probs_T(eng, t, c, opening, lambda a, b: nc.scalar.activation(a, b, ACT.Copy))
                    if c < CHUNKS - 1:
                        exps(t, p, c + 1, opening)
                    elif not closing:
                        exps(t + 1, 1 - p, 0, False)
                    if c == 2 and not closing:
                        heads_T_first(t + 1, 1 - p)
                    if c == 2 and not opening:
                        heads_out_T(t - 1, 1, False)
                    if c == 6:
                        heads_out_T(t, 0, False)
            tiles(eng, tile_first, lambda t, n, p: heads_out_T(t, 1, True), 0)
            end(eng)
            begin(eng, 2)
            for k in range(3):
                split(0, k, True)
            lnT(1)
            end(eng)
            stage[0] = LAYER
            begin(eng, 3)

            def start(t0, part):
                if part == 0:
                    copy_input(0, 0, True)
                if part == 1:
                    square(t0, 0, True)
                    square(t0, 1, True)
                if part == 2:
                    square(t0, 2, True)
                    values(t0, 0, 0)
                if part == 3:
                    heads_T(t0, 0, 0)
                    heads_T(t0, 0, 1)
                    square(t0, 3, True)
                    values(t0, 0, 1)
                    exps(t0, 0, 0, True)

            def layer(l, last):
                t0 = TILES + l * TILES

                def tile(t, n, p, opening, closing):
                    if not closing:
                        copy_input(n + 1, 1 - p, True)
                    for c in range(CHUNKS):
                        if c in ACT_COPIES:
                            probs_T(eng, t, c, opening, lambda a, b: nc.scalar.activation(a, b, ACT.Copy))
                        if c < CHUNKS - 1:
                            exps(t, p, c + 1, opening)
                        elif not closing:
                            exps(t + 1, 1 - p, 0, False)
                        if c == 0 and opening:
                            heads_T(t, p, 2)
                        if c == 1:
                            heads_T(t, p, 3)
                        if not closing:
                            if c in HEADS_T and c in HEADS_FIRST:
                                heads_T(t + 1, 1 - p, HEADS_T[c])
                            if c in SQUARE:
                                square(t + 1, SQUARE[c])
                            if c in VALUES:
                                values(t + 1, 1 - p, VALUES[c])
                            if c in HEADS_T and c not in HEADS_FIRST:
                                heads_T(t + 1, 1 - p, HEADS_T[c])
                        if c == 2 and not opening:
                            heads_out_T(t - 1, 1, False)
                        if c == 6:
                            heads_out_T(t, 0, False)
                        if closing and c in (1, 3):
                            shifted(l, c // 2)
                        if closing and c == 7:
                            normed_T(0)


                def normed_T(s):
                    F = l * SUPERS + s
                    if s == 0:
                        eng.wait_ge(ffn_loaded, (l + 1) * 48)
                    eng.wait_ge(f_t2, F + 1)
                    if s >= 2:
                        eng.wait_ge(f_up, (F - 1) * 3)
                    nc.scalar.activation(xnT[:, s % 2, :], T2[:, :], ACT.Identity, scale=vec[:, 0:1],
                                         bias=vec[:, 1:2]).then_inc(f_xnT, 1)

                def gate(s, i):
                    m = FF_CHUNKS[i][1]
                    k, r = (l * SUPERS + s) * 3 + i, (s * 3 + i) % 2
                    eng.wait_ge(f_gate, k + 1)
                    if s * 3 + i >= 2:
                        eng.wait_ge(f_hid, k - 1)
                    nc.scalar.activation(gl[0:m, r, :], GATE[r][0:m, :], ACT.Gelu,
                                         bias=vec[0:m, 5 + i:6 + i]).then_inc(f_act, 1)

                def close(t, n, p):
                    gate(0, 0)
                    heads_out_T(t, 1, True)
                    normed_T(1)
                tiles(eng, tile, close, t0)
                for s in range(SUPERS):
                    if s + 2 < SUPERS:
                        shifted(l, s + 2)
                    elif s == 2 and not last:
                        eng.wait_ge(f_out, l * SUPERS + 1)
                        start(t0 + TILES, 0)
                    gate(s, 1)
                    if s == 0 and not last:
                        split(l + 1, 0)
                    if s in (1, 2):
                        normed_T(s + 1)
                    gate(s, 2)
                    if s == 0 and not last:
                        split(l + 1, 1)
                    if s == 2 and not last:
                        start(t0 + TILES, 1)
                    if s + 1 < SUPERS:
                        gate(s + 1, 0)
                    if s == 0 and not last:
                        split(l + 1, 2)
                    if s == 2 and not last:
                        start(t0 + TILES, 2)
                if not last:
                    start(t0 + TILES, 3)
            for part in range(4):
                start(TILES, part)
            with eng.Fori(0, DEPTH - 1) as l:
                layer(l, False)
            layer(DEPTH - 1, True)
            for s in range(SUPERS):
                eng.wait_ge(lnT_full, 2 * SUPERS + s + 1)
                nc.scalar.activation(y_nat[:, s * SUPER:(s + 1) * SUPER, :],
                                     bank[s][:, :].rearrange("p (t q) -> p t q", t=SUPER), ACT.Copy
                                     ).then_inc(lnT_free, 1)

        @block.vector
        def _(eng):
            def norms(src, k, tl=range(TILES)):
                for n in tl:
                    last = nc.vector.bn_stats(stats[:, n, :], src[:, n, :])
                last.then_inc(f_st, 1)
                eng.wait_ge(f_st, fst[0])
                fst[0] += 1
                for n in tl:
                    last = nc.vector.bn_aggr(mv[:, n, :], stats[:, n, :])
                last.then_inc(f_st, 1)
                eng.wait_ge(f_st, fst[0])
                fst[0] += 1
                nc.vector.tensor_scalar(veps[:, :], mv[:, :, 1], EPS, None, ALU.add).then_inc(ln_step, 1)
                eng.wait_ge(ln_pow, k + 1)
                for n in tl:
                    last = nc.vector.tensor_scalar(ln_nat[:, n, :], src[:, n, :], mv[:, n, 0:1], rstd[:, n:n + 1],
                                                   ALU.subtract, ALU.mult)
                last.then_inc(ln_step, 1)

            fst = [1]

            def maxima(t, p, c):
                G, r = t * 8 + c, c % 2
                eng.wait_ge(s_ready, G + 1)
                if c == 0:
                    at_least(eng, p_ready, (t - 1) * 8)
                nc.vector.tensor_reduce(nmax[:, p, 2 * c:2 * c + 2],
                                        SB[r][:, 0:2 * P].rearrange("p (h k) -> p h k", h=2),
                                        AX.X, ALU.max, negate=True).then_inc(max_ready, 1)

            def heads_out(t, p, half):
                H, w = t * 2 + half, stage[0].K
                eng.wait_ge(pv_done, t * 8 + 4 * half + 4)
                hs = slice(8 * half, 8 * half + 8)
                nc.vector.reciprocal(linv[:, p, hs], lsum[:, p, hs]).then_inc(linv_ready, 1)
                eng.wait_ge(linv_ready, H + 1)
                nc.vector.tensor_tensor(
                    o_nat[:, half, 0:w * 8].rearrange("p (h d) -> p h d", d=w),
                    OB[:, 0:w * 8].rearrange("p (h d) -> p h d", d=w),
                    linv[:, p, hs].rearrange("p (h o) -> p h o", o=1).to_broadcast([P, 8, w]),
                    ALU.mult).then_inc(o_evac, 1)

            def residual(t, n):
                eng.wait_ge(wo_done, t * 2 + 2)
                if stage[0].first:
                    nc.vector.tensor_tensor(y_nat[:, n, :], YB[:, 0:C], bias_p[:, :], ALU.add).then_inc(y_free, 1)
                else:
                    nc.vector.tensor_tensor(xB[:, n + 1, 0:1], YB[:, P - 1:P], xA[:, n, P:P + 1], ALU.add)
                    nc.vector.tensor_tensor(xB[:, n, 1:P + 1], YB[:, 0:P], xA[:, n, 1:P + 1], ALU.add
                                            ).then_inc(y_free, 1)

            def copy_prev(t, n, p):
                at_least(eng, s_ready, (t - 1) * 8)
                at_least(eng, pv_done, (t - 1) * 8)
                nc.vector.tensor_scalar(kT[:, p, :, 0:WIN], kT[:, 1 - p, :, P:KEYS], follows[:, bass.ds(n, 1)], None,
                                        ALU.mult).then_inc(prev_ready, 1)
                nc.vector.tensor_copy(vlow[P - WIN:P, p, :], v[P - WIN:P, 1 - p, :]).then_inc(prev_ready, 1)

            def input_rest(t, n, p):
                eng.wait_ge(xs_ready, t * 2 + 2)
                for a, rows in ((1, slice(0, C // 2)), (0, slice(C // 2, C))):
                    nc.vector.tensor_tensor(xs_lo[rows, p, :], xA[rows, n, a:P + a], xs[rows, p, :].bitcast(f32),
                                            ALU.subtract).then_inc(xs_rest, 1)

            def rotary(t, n, j, fresh=False):
                i = t - TILES
                Q, r, pj = i * 4 + j, j % 2, PJ[QK_AT[j] % 2]
                eng.wait_ge(pj_act, i * 6 + QK_AT[j] + 1)
                if not (fresh and j < 2):
                    eng.wait_ge(w_ready, Q - 1)
                heads3 = "p (h d) -> p h d"
                nc.vector.tensor_reduce(n2[:, r, :], sq[:, r, :].rearrange(heads3, d=D), AX.X, ALU.add
                                        ).then_inc(n2_ready, 1)
                k = 2 * (j % 2)
                nc.vector.tensor_tensor(
                    tc_[:, r, :].rearrange(heads3, d=D), pj[:, :].rearrange(heads3, d=D),
                    ropeL[:, k, n, :].rearrange("p (o d) -> p o d", o=1).to_broadcast([P, 8, D]), ALU.mult)
                eng.wait_ge(n2_ready, Q + 1)
                nc.vector.tensor_scalar(n2c[:, r, :], n2[:, r, :], 1e-24, None, ALU.max).then_inc(n2c_ready, 1)
                for a in range(2):
                    lo, hi = a * (D // 2), (1 - a) * (D // 2)
                    last = nc.vector.tensor_tensor(
                        ts_[:, r, :].rearrange(heads3, d=D)[:, :, lo:lo + D // 2],
                        pj[:, :].rearrange(heads3, d=D)[:, :, hi:hi + D // 2],
                        ropeL[:, k + 1, n, lo:lo + D // 2].rearrange("p (o d) -> p o d", o=1
                                                                     ).to_broadcast([P, 8, D // 2]), ALU.mult)
                last.then_inc(pj_dve, 1)

            def qkv_first(t, p):
                eng.wait_ge(a_pj, t + 1)
                at_least(eng, tp_free, t)
                at_least(eng, pv_done, (t - 1) * 8)
                at_least(eng, prev_ready, t * 2)
                nc.vector.tensor_tensor(w_nat[:, 0, 0:2 * C], PJ[0][:, 0:2 * C], bias_a[:, 0:2 * C], ALU.add
                                        ).then_inc(a_qkv, 1)
                lo = P - WIN
                nc.vector.tensor_tensor(vlow[0:lo, p, 0:C], PJ[0][0:lo, 2 * C:3 * C], bias_a[0:lo, 2 * C:3 * C], ALU.add)
                nc.vector.tensor_tensor(v[:, p, 0:C], PJ[0][:, 2 * C:3 * C], bias_a[:, 2 * C:3 * C], ALU.add
                                        ).then_inc(a_qkv, 1)

            stage = [FIRST]
            eng.wait_ge(x_loaded, 16 * SUPERS)
            norms(x_nat, 0)
            end(eng)
            begin(eng, 1)
            eng.wait_ge(c_loaded, CONSTS)
            copy_prev(0, 0, 0)
            qkv_first(0, 0)
            maxima(0, 0, 0)
            maxima(0, 0, 1)

            def tile_first(t, n, p, opening, closing):
                for c in range(CHUNKS):
                    if c == 1 and not opening:
                        heads_out(t - 1, 1 - p, 1)
                    if c == 5:
                        heads_out(t, p, 0)
                    if c not in LATE and c not in ACT_COPIES:
                        probs_T(eng, t, c, opening, nc.vector.tensor_copy)
                    if c < CHUNKS - 2:
                        maxima(t, p, c + 2)
                    elif not closing:
                        maxima(t + 1, 1 - p, c + 2 - CHUNKS)
                    if c in LATE and c not in ACT_COPIES:
                        probs_T(eng, t, c, opening, nc.vector.tensor_copy)
                    if c == 1 and not closing:
                        qkv_first(t + 1, 1 - p)
                    if c == 3 and not closing:
                        eng.wait_ge(tp_free, t + 1)
                        eng.wait_ge(a_qkv, t * 2 + 2)
                        copy_prev(t + 1, n + 1, 1 - p)
                    if c == 4 and not opening:
                        residual(t - 1, n - 1)

            def close(t, n, p):
                heads_out(t, p, 1)
                residual(t, n)
            tiles(eng, tile_first, close, 0)
            end(eng)
            begin(eng, 2)
            norms(y_nat, 1)
            eng.wait_ge(ln_step, 4)
            for n in range(TILES):
                last = nc.vector.tensor_tensor(x_nat[:, n, :], x_nat[:, n, :], ln_nat[:, n, :], ALU.add)
            last.then_inc(f_st, 1)
            eng.wait_ge(f_st, fst[0])
            fst[0] += 1
            norms(x_nat, 2)
            end(eng)
            stage[0] = LAYER
            base_st = fst[0] - 1
            begin(eng, 3)

            def start(l, part):
                t0 = TILES + l * TILES
                if part == 0:
                    input_rest(t0, 0, 0)
                if part == 1:
                    eng.wait_ge(rope_ready, l * 4 + 4)
                    rotary(t0, 0, 0, True)
                if part == 2:
                    rotary(t0, 0, 1, True)
                if part == 3:
                    rotary(t0, 0, 2, True)
                if part == 4:
                    copy_prev(t0, 0, 0)
                if part == 5:
                    maxima(t0, 0, 0)
                    maxima(t0, 0, 1)
                    rotary(t0, 0, 3, True)

            def layer(l, last):
                t0 = TILES + l * TILES

                def norm_stats(s):
                    F = l * SUPERS + s
                    eng.wait_ge(f_t1, F + 1)
                    for j in range(SUPER):
                        last = nc.vector.bn_stats(stats[:, j, :], T1[s % 2][:, j * C:(j + 1) * C])
                    eng.drain()
                    for j in range(SUPER):
                        last = nc.vector.bn_aggr(mv[:, j, :], stats[:, j, :])
                    last.then_inc(f_st, 1)
                    eng.wait_ge(f_st, F + 1 + base_st)
                    nc.vector.tensor_scalar(veps[:, 0:SUPER], mv[:, 0:SUPER, 1], EPS, None, ALU.add).then_inc(f_eps, 1)

                def norm(s):
                    F = l * SUPERS + s
                    eng.wait_ge(f_pow, F + 1)
                    if s:
                        eng.wait_ge(f_t2, F)
                    for j in range(SUPER):
                        last = nc.vector.tensor_scalar(xn[:, j, :], T1[s % 2][:, j * C:(j + 1) * C], mv[:, j, 0:1],
                                                       rstd[:, j:j + 1], ALU.subtract, ALU.mult)
                    last.then_inc(f_xn, 1)

                def hidden(s, i):
                    m = FF_CHUNKS[i][1]
                    k, r = (l * SUPERS + s) * 3 + i, (s * 3 + i) % 2
                    eng.wait_ge(f_act, k + 1)
                    eng.wait_ge(f_up, k + 1)
                    nc.vector.scalar_tensor_tensor(hid[0:m, s % 2, i, :], UP[r][0:m, :], vec[0:m, 2 + i:3 + i],
                                                   gl[0:m, r, :], ALU.add, ALU.mult).then_inc(f_hid, 1)

                def output(s):
                    eng.wait_ge(f_down, l * SUPERS + s + 1)
                    y4 = DOWN[:, :].rearrange("p (t q) -> p t q", t=SUPER)
                    t4 = slice(s * SUPER, (s + 1) * SUPER)
                    nc.vector.scalar_tensor_tensor(xA[:, s * SUPER + 1:(s + 1) * SUPER + 1, 0:1], y4[:, :, P - 1:P],
                                                   vec[:, 8:9], xB[:, t4, P:P + 1], ALU.add, ALU.add)
                    nc.vector.scalar_tensor_tensor(xA[:, t4, 1:P + 1], y4, vec[:, 8:9], xB[:, t4, 1:P + 1],
                                                   ALU.add, ALU.add).then_inc(f_out, 1)

                def tile(t, n, p, opening, closing):
                    if not closing:
                        input_rest(t + 1, n + 1, 1 - p)
                    for c in range(CHUNKS):
                        if c == 1 and not opening:
                            heads_out(t - 1, 1 - p, 1)
                        if c == 5:
                            heads_out(t, p, 0)
                        if c not in LATE and c not in ACT_COPIES:
                            probs_T(eng, t, c, opening, nc.vector.tensor_copy)
                        if c < CHUNKS - 2:
                            maxima(t, p, c + 2)
                        elif not closing:
                            maxima(t + 1, 1 - p, c + 2 - CHUNKS)
                        if c in LATE and c not in ACT_COPIES:
                            probs_T(eng, t, c, opening, nc.vector.tensor_copy)
                        if c in ROTARY and not closing:
                            rotary(t + 1, n + 1, ROTARY[c])
                        if c == COPY_PREV and not closing:
                            eng.wait_ge(pj_act, (t - TILES) * 6 + 6)
                            eng.wait_ge(tp_free, TILES + (t - TILES) * 4 + 4)
                            copy_prev(t + 1, n + 1, 1 - p)
                        if c == RESIDUAL and not opening:
                            residual(t - 1, n - 1)
                        if closing and c in (5, 7):
                            norm_stats(c // 6)
                        if closing and c == 6:
                            norm(0)

                def close(t, n, p):
                    eng.wait_ge(y_free, t0 + PER_SEQ)
                    nc.vector.memset(xB[:, PER_SEQ, 0:1], 0.0).then_inc(edge, 1)
                    heads_out(t, p, 1)
                    norm(1)
                    residual(t, n)
                tiles(eng, tile, close, t0)
                eng.wait_ge(ffn_loaded, (l + 1) * 48)
                hidden(0, 0)
                for s in range(SUPERS):
                    if s == 2 and not last:
                        start(l + 1, 0)
                    hidden(s, 1)
                    if s + 2 < SUPERS:
                        norm_stats(s + 2)
                    elif s == 3 and not last:
                        start(l + 1, 3)
                    hidden(s, 2)
                    if s == 2 and not last:
                        start(l + 1, 1)
                    if s + 1 < SUPERS:
                        hidden(s + 1, 0)
                    if s + 2 < SUPERS:
                        norm(s + 2)
                    if s == 2 and not last:
                        start(l + 1, 2)
                    if s == 3 and not last:
                        start(l + 1, 4)
                    output(s)
                    if s == 2:
                        eng.wait_ge(f_out, l * SUPERS + 2)
                        nc.vector.memset(xA[:, PER_SEQ, 0:1], 0.0)
                if not last:
                    start(l + 1, 5)
            for part in range(6):
                start(0, part)
            with eng.Fori(0, DEPTH - 1) as l:
                layer(l, False)
            layer(DEPTH - 1, True)
            eng.wait_ge(lnT_free, SUPERS)
            for n in range(TILES):
                last = nc.vector.bn_stats(stats[:, n, :], y_nat[:, n, :])
            last.then_inc(f_st, 1)
            at = base_st + DEPTH * SUPERS
            eng.wait_ge(f_st, at + 1)
            for n in range(TILES):
                last = nc.vector.bn_aggr(mv[:, n, :], stats[:, n, :])
            last.then_inc(f_st, 1)
            eng.wait_ge(f_st, at + 2)
            nc.vector.tensor_scalar(veps[:, :], mv[:, :, 1], EPS, None, ALU.add).then_inc(ln_step, 1)
            eng.wait_ge(ln_pow, 4)
            for n in range(TILES):
                last = nc.vector.tensor_scalar(ln_nat[:, n, :], y_nat[:, n, :], mv[:, n, 0:1], rstd[:, n:n + 1],
                                               ALU.subtract, ALU.mult)
            last.then_inc(f_st, 1)
            eng.wait_ge(f_st, at + 3)
            for s in range(SUPERS):
                t4 = slice(s * SUPER, (s + 1) * SUPER)
                nc.vector.tensor_tensor(x_nat[:, t4, :], x_nat[:, t4, :], ln_nat[:, t4, :], ALU.add).then_inc(out_ready, 1)

        @block.tensor
        def _(eng):
            def transposes(src, k):
                for s in range(SUPERS):
                    for j in range(SUPER):
                        last = nc.tensor.transpose(bank[s][:, j * P:(j + 1) * P], src(s * SUPER + j), idf[:, :])
                    last.then_inc(lnT_full, 1)

            def scores(t, n, p, c):
                st = stage[0]
                G, r = t * 8 + c, c % 2
                base, pair = st.heads(c)
                if c == 0:
                    eng.wait_ge(tp_free, t + 1 if st.first else TILES + (t - TILES) * 4 + 2)
                    eng.wait_ge(prev_ready, t * 2 + 2)
                if st.first:
                    eng.wait_ge(k_each, t * CHUNKS + c + 1)
                if c == 4 and not st.first:
                    eng.wait_ge(tp_free, TILES + (t - TILES) * 4 + 4)
                at_least(eng, p_ready, G - 1)
                nc.tensor.matmul(SB[r][:, 0:2 * P], idb[:, :].bitcast(bf16),
                                 msk[:, n, :].bitcast(bf16).rearrange("p (o k) -> p o k", o=1).to_broadcast([P, 2, P]),
                                 start=True, stop=False, skip_group_check=True)
                q, k = [], []
                for g, head in pair:
                    q.append(qT[:, p, 0, :] if st.first else qT[base:base + D, p, g, :])
                    k.append(kEach[:, p, g, :] if st.first else kT[base:base + D, p, g, :])
                for h in range(2):
                    nc.tensor.matmul(SB[r][0:HALF, h * P:h * P + HALF], q[h][:, 0:HALF], k[h][:, WIN:WIN + HALF],
                                     start=False, stop=True, skip_group_check=True)
                    nc.tensor.matmul(SB[r][HALF:P, h * P + WIN:(h + 1) * P], q[h][:, HALF:P], k[h][:, 2 * WIN:KEYS],
                                     start=False, stop=True, skip_group_check=True)
                for h in range(2):
                    last = nc.tensor.matmul(SB[r][0:WIN, (h + 1) * P - WIN:(h + 1) * P], q[h][:, 0:WIN], k[h][:, 0:WIN],
                                            start=False, stop=True, skip_group_check=True)
                last.then_inc(s_ready, 1)

            def transpose_probs(t, c, opening):
                G, r = t * 8 + c, c % 2
                eng.wait_ge(p_ready, G + 1)
                at_least(eng, pt_free, turn(t, c, opening))
                for h in range(2):
                    last = nc.tensor.transpose(PT[:, h * P:(h + 1) * P], prob[:, r, h, :], idf[:, :])
                last.then_inc(pt_full, 1)

            def weigh_values(t, p, c, opening):
                st = stage[0]
                eng.wait_ge(pt_free, turn(t, c, opening) + 1)
                if c == 0:
                    at_least(eng, o_evac, t * 2)
                    if st.first:
                        eng.wait_ge(a_qkv, t * 2 + 2)
                    else:
                        eng.wait_ge(pj_act, (t - TILES) * 6 + V_AT[0] + 1)
                if c == 4:
                    eng.wait_ge(o_evac, t * 2 + 1)
                    if not st.first:
                        eng.wait_ge(pj_act, (t - TILES) * 6 + V_AT[1] + 1)
                r = c % 2
                for h, (g, head) in enumerate(st.heads(c)[1]):
                    a, vc = st.column(head), slice(head * st.K, (head + 1) * st.K)
                    nc.tensor.matmul(OB[0:HALF, a:a + st.K], pT[:, r, h, 0:HALF], vlow[:, p, vc], start=True, stop=True,
                                     skip_group_check=True)
                    last = nc.tensor.matmul(OB[HALF:P, a:a + st.K], pT[:, r, h, HALF:P], v[:, p, vc],
                                            start=True, stop=True, skip_group_check=True)
                last.then_inc(pv_done, 1)

            def project(t, p, x, fresh=False):
                i = t - TILES
                if x == 0:
                    eng.wait_ge(xs_rest, (t - TILES) * 2 + 2)
                if not (fresh and x < 2):
                    eng.wait_ge(pj_act, i * 6 + x - 1)
                    if x in (0, 2, 3, 4):
                        eng.wait_ge(pj_dve, i * 4 + {0: 0, 2: 1, 3: 2, 4: 3}[x])
                col = [0, INNER, HB, 2 * INNER, INNER + HB, 2 * INNER + HB][x]
                hi, rest = w_hi[:, col:col + HB], w_lo[:, col:col + HB]
                nc.tensor.matmul(PJ[x % 2][:, :], xs[:, p, :], hi, start=True, stop=False)
                nc.tensor.matmul(PJ[x % 2][:, :], xs[:, p, :], rest, start=False, stop=False)
                nc.tensor.matmul(PJ[x % 2][:, :], xs_lo[:, p, :], hi, start=False, stop=True).then_inc(pj_ready, 1)

            def transpose_heads(t, j):
                Q = (t - TILES) * 4 + j
                eng.wait_ge(w_ready, Q + 1)
                eng.wait_ge(tp_free, TILES + Q)
                for i in range(4):
                    last = nc.tensor.transpose(TP[:, i * P:(i + 1) * P], w_nat[:, j % 2, i * P:(i + 1) * P], idf[:, :])
                last.then_inc(tp_full, 1)

            def project_first(t, p):
                eng.wait_ge(xs_ready, t * 2 + 2)
                at_least(eng, a_qkv, t * 2)
                nc.tensor.matmul(PJ[0][:, 0:3 * C], xs0[:, p, :], wa[:, :], start=True, stop=True).then_inc(a_pj, 1)

            def transpose_first(t):
                eng.wait_ge(a_qkv, t * 2 + 1)
                at_least(eng, tp_free, t)
                for i in range(2):
                    last = nc.tensor.transpose(TP[:, i * P:(i + 1) * P], w_nat[:, 0, i * P:(i + 1) * P], idf[:, :])
                last.then_inc(tp_full, 1)

            def transpose_out(t, half, closing):
                eng.wait_ge(o_evac, t * 2 + half + 1)
                eng.wait_ge(pt_free, out_turn(t, half, closing))
                for i in range(1 if stage[0].first else 4):
                    last = nc.tensor.transpose(PT[:, i * P:(i + 1) * P], o_nat[:, half, i * P:(i + 1) * P], idf[:, :])
                last.then_inc(pt_full, 1)

            def project_out(t, half, closing):
                eng.wait_ge(pt_free, out_turn(t, half, closing) + 1)
                if half == 0:
                    at_least(eng, y_free, t)
                if stage[0].first:
                    nc.tensor.matmul(YB[:, 0:C], oT[0:C // 2, half, 0:P], wp[:, half, :], start=half == 0,
                                     stop=half == 1).then_inc(wo_done, 1)
                    return
                for i in range(4):
                    last = nc.tensor.matmul(YB[:, 0:P], wo[:, 4 * half + i, :], oT[:, half, i * P:(i + 1) * P],
                                            start=half == 0 and i == 0, stop=half == 1 and i == 3)
                last.then_inc(wo_done, 1)

            def heads_transposes(t, p, c, opening, closing):
                if not stage[0].first:
                    if c == 0 and opening:
                        transpose_heads(t, 2)
                    if c == 1:
                        transpose_heads(t, 3)
                    if not closing and c in HEADS_T:
                        transpose_heads(t + 1, HEADS_T[c])

            def chunk(t, n, p, c, opening, closing):
                if c not in LATE:
                    transpose_probs(t, c, opening)
                if c in (2, 6):
                    weigh_values(t, p, c - 1, opening)
                if c < CHUNKS - 2:
                    scores(t, n, p, c + 2)
                elif not closing:
                    scores(t + 1, n + 1, 1 - p, c + 2 - CHUNKS)
                if c in HEADS_FIRST:
                    heads_transposes(t, p, c, opening, closing)
                if stage[0].first:
                    if not closing:
                        if c == 0:
                            project_first(t + 1, 1 - p)
                        if c == 2:
                            transpose_first(t + 1)
                else:
                    if not closing and c in PROJECT:
                        project(t + 1, 1 - p, PROJECT[c])
                if c not in (0, 2, 6):
                    weigh_values(t, p, c - 1, opening)
                if c == 0 and not opening:
                    weigh_values(t - 1, 1 - p, CHUNKS - 1, False)
                if c in LATE:
                    transpose_probs(t, c, opening)
                if c not in HEADS_FIRST:
                    heads_transposes(t, p, c, opening, closing)
                if not opening:
                    if c == 2:
                        transpose_out(t - 1, 1, False)
                    if c == 3:
                        project_out(t - 1, 1, False)
                if c == 6:
                    transpose_out(t, 0, False)
                if c == 7:
                    project_out(t, 0, False)

            def tile(t, n, p, opening, closing):
                for c in range(CHUNKS):
                    chunk(t, n, p, c, opening, closing)

            def close(t, n, p):
                weigh_values(t, p, CHUNKS - 1, False)
                transpose_out(t, 1, True)
                project_out(t, 1, True)

            stage = [FIRST]
            eng.wait_ge(c_loaded, CONSTS)
            eng.wait_ge(ln_step, 2)
            transposes(lambda n: ln_nat[:, n, :], 0)
            end(eng)
            begin(eng, 1)
            project_first(0, 0)
            transpose_first(0)
            scores(0, 0, 0, 0)
            scores(0, 0, 0, 1)

            tiles(eng, tile, close, 0)
            end(eng)
            begin(eng, 2)
            eng.wait_ge(ln_step, 6)
            transposes(lambda n: ln_nat[:, n, :], 1)
            end(eng)
            stage[0] = LAYER
            begin(eng, 3)

            def start(l, part):
                t0 = TILES + l * TILES
                if part == 0:
                    eng.wait_ge(w_rest, l * 3 + 3)
                    project(t0, 0, 0, True)
                    project(t0, 0, 1, True)
                if part == 1:
                    project(t0, 0, 2, True)
                    project(t0, 0, 3, True)
                if part == 2:
                    transpose_heads(t0, 0)
                if part == 3:
                    transpose_heads(t0, 1)
                    scores(t0, 0, 0, 0)
                    scores(t0, 0, 0, 1)
                    project(t0, 0, 4, True)
                    project(t0, 0, 5, True)

            def layer(l, last):
                t0 = TILES + l * TILES

                def transpose_in(s):
                    F = l * SUPERS + s
                    eng.wait_ge(f_x, F * 2 + 2)
                    for j in range(SUPER):
                        last = nc.tensor.transpose(T1[s % 2][:, j * C:(j + 1) * C], xf[:, s % 2, j, :], idf[:, :])
                    last.then_inc(f_t1, 1)

                def transpose_normed(s):
                    eng.wait_ge(f_xn, l * SUPERS + s + 1)
                    for j in range(SUPER):
                        last = nc.tensor.transpose(T2[:, j * P:(j + 1) * P], xn[:, j, :], idf[:, :])
                    last.then_inc(f_t2, 1)

                def gate_up(s, i):
                    a, m = FF_CHUNKS[i]
                    F, r = l * SUPERS + s, (s * 3 + i) % 2
                    if s == 0 and i == 0:
                        eng.wait_ge(ffn_loaded, (l + 1) * 48)
                    if i == 0:
                        eng.wait_ge(f_xnT, F + 1)
                    if s * 3 + i >= 2:
                        eng.wait_ge(f_hid, F * 3 + i - 1)
                    nc.tensor.matmul(GATE[r][0:m, :], w1[:, FF + a:FF + a + m], xnT[:, s % 2, :], start=True, stop=True
                                     ).then_inc(f_gate, 1)
                    nc.tensor.matmul(UP[r][0:m, :], w1[:, a:a + m], xnT[:, s % 2, :], start=True, stop=True
                                     ).then_inc(f_up, 1)

                def down(s):
                    F = l * SUPERS + s
                    eng.wait_ge(f_hid, F * 3 + 3)
                    if s:
                        eng.wait_ge(f_out, F)
                    else:
                        eng.wait_ge(y_free, t0 + TILES)
                    for i, (_, m) in enumerate(FF_CHUNKS):
                        last = nc.tensor.matmul(DOWN[:, :], w2[0:m, i, :], hid[0:m, s % 2, i, :], start=i == 0, stop=i == 2)
                    last.then_inc(f_down, 1)

                def tile_and_norm(t, n, p, opening, closing):
                    for c in range(CHUNKS):
                        chunk(t, n, p, c, opening, closing)
                        if closing and c == 3:
                            transpose_in(0)
                        if closing and c == 6:
                            transpose_in(1)
                        if closing and c == 7:
                            transpose_normed(0)

                def close_layer(t, n, p):
                    weigh_values(t, p, CHUNKS - 1, False)
                    gate_up(0, 0)
                    transpose_out(t, 1, True)
                    transpose_normed(1)
                    project_out(t, 1, True)
                eng.wait_ge(wo_loaded, (l + 1) * 16)
                tiles(eng, tile_and_norm, close_layer, t0)
                for s in range(SUPERS):
                    gate_up(s, 1)
                    if s + 2 < SUPERS:
                        transpose_in(s + 2)
                    if s in (1, 2):
                        transpose_normed(s + 1)
                    gate_up(s, 2)
                    if s == 2 and not last:
                        start(l + 1, 0)
                    if s == 3 and not last:
                        start(l + 1, 2)
                    if s + 1 < SUPERS:
                        gate_up(s + 1, 0)
                    down(s)
                    if s == 2 and not last:
                        start(l + 1, 1)
                if not last:
                    start(l + 1, 3)
            for part in range(4):
                start(0, part)
            with eng.Fori(0, DEPTH - 1) as l:
                layer(l, False)
            layer(DEPTH - 1, True)
            eng.wait_ge(f_out, DEPTH * SUPERS)
            transposes(lambda n: xA[:, n, 1:P + 1], 2)


def _constants():
    import numpy as np
    f = np.float32
    half = np.arange(0, D, 2, dtype=f)
    inv_freq = (f(1.0) / f(10000.0) ** (half / f(D))).astype(f)
    t = np.arange(N, dtype=f)
    freqs = t[:, None] * inv_freq[None, :]
    freqs = np.concatenate([freqs, freqs], -1)
    base = (half + f(0.4 * D)) / f(1.4 * D)
    scale = base[None, :] ** ((t - f(N // 2)) / f(WIN // 2))[:, None]
    scale = np.concatenate([scale, scale], -1).astype(f)
    cos, sin = np.cos(freqs), np.sin(freqs)
    sign = np.concatenate([-np.ones(D // 2, f), np.ones(D // 2, f)])
    inv = f(1.0) / scale
    tabs = np.stack([cos * scale, sin * sign * scale, cos * inv * f(8), sin * sign * inv * f(8)])
    rope = tabs.reshape(4, PER_SEQ, P, D).transpose(2, 0, 1, 3).astype(f)
    i = np.arange(P)[:, None]
    j = np.arange(P)[None, :]
    own = (j <= i) & (j >= i - WIN)
    before = (i < HALF) & (j >= P - WIN) & (j - P >= i - WIN)
    tile = np.arange(TILES)[:, None, None] % PER_SEQ
    ok = own[None] | (before[None] & (tile > 0))
    mask = np.where(ok, 0.0, -1e30).transpose(1, 0, 2).astype(f)
    eye = np.eye(P, dtype=f)

    def bf16_bits(a):
        return (np.ascontiguousarray(a).view(np.uint32) >> 16).astype(np.uint16)
    return np.ascontiguousarray(rope), eye, bf16_bits(eye), bf16_bits(mask)


def kernel(L0_attn_x, L0_attn_W_attn, L0_attn_b_attn, L0_attn_W_proj, L0_attn_b_proj, L0_ffn_Wqkv, L0_ffn_q_scale,
           L0_ffn_k_scale, L0_ffn_Wo, L0_ffn_ln_g, L0_ffn_ln_b, L0_ffn_W1, L0_ffn_b1, L0_ffn_W2, L0_ffn_b2):
    import numpy as np
    import concourse.bacc as bacc
    from concourse.bass_utils import run_bass_kernel_spmd

    A = np.ascontiguousarray
    rope, eye, eyeb, mask = _constants()

    def swap(s):
        return np.concatenate([s[:, D // 2:], s[:, :D // 2]], -1)
    qs, ks = np.asarray(L0_ffn_q_scale), np.asarray(L0_ffn_k_scale)
    scales = np.stack([qs, swap(qs), ks, swap(ks)], 1)
    scales = A(np.broadcast_to(scales[:, None], (DEPTH, P, 4, D)))
    par = np.zeros((DEPTH, P, PAR), np.float32)
    b1 = np.asarray(L0_ffn_b1)
    par[:, :, 0], par[:, :, 1], par[:, :, 8] = np.asarray(L0_ffn_ln_g), np.asarray(L0_ffn_ln_b), np.asarray(L0_ffn_b2)
    for i, (a, m) in enumerate(FF_CHUNKS):
        par[:, :m, 2 + i] = b1[:, a:a + m]
        par[:, :m, 5 + i] = b1[:, FF + a:FF + a + m]
    w2 = np.zeros((DEPTH, 3 * P, C), np.float32)
    w2[:, :FF] = np.asarray(L0_ffn_W2)
    ins = {
        "x": A(np.asarray(L0_attn_x).reshape(B * N, C)), "w_attn": A(L0_attn_W_attn),
        "b_attn": A(np.broadcast_to(np.asarray(L0_attn_b_attn), (P, 3 * C))), "w_proj": A(L0_attn_W_proj),
        "b_proj": A(np.broadcast_to(np.asarray(L0_attn_b_proj), (P, C))), "w_qkv": A(L0_ffn_Wqkv),
        "w_o": A(L0_ffn_Wo), "scales": scales, "w_1": A(L0_ffn_W1), "w_2": w2, "vectors": par, "rope": rope,
        "identity": eye, "identity_bf16": eyeb, "mask": mask, "select": np.repeat(np.eye(HEADS, dtype=np.float32), DA, 0),
    }
    nc = bacc.Bacc("TRN2", target_bir_lowering=False, num_devices=1)
    aps = [nc.dram_tensor(k, a.shape, mybir.dt.from_np(a.dtype), kind="ExternalInput").ap() for k, a in ins.items()]
    out = nc.dram_tensor("out", (B * N, C), mybir.dt.float32, kind="ExternalOutput").ap()
    build(nc, *aps, out)
    r = run_bass_kernel_spmd(nc, [ins], core_ids=[0])
    return r.results[0]["out"].reshape(B, N, C)
```
